# Optimizing a Trainium2 kernel written in Bass

```python
import numpy as np
import jax
import jax.numpy as jnp

def _softmax(x, axis=-1):
    return jax.nn.softmax(x, axis=axis)

def _gelu(x):
    return jax.nn.gelu(x, approximate=True)

def _silu(x):
    return jax.nn.silu(x)

def _sigmoid(x):
    return jax.nn.sigmoid(x)

def _layernorm(x, axis=-1, eps=1e-05):
    m = jnp.mean(x, axis=axis, keepdims=True)
    v = jnp.var(x, axis=axis, keepdims=True)
    return (x - m) / jnp.sqrt(v + eps)

def _scatter_add(tgt, idx, src, axis=0):
    return tgt.at[idx].add(src)

def _segment_sum(src, seg, n):
    return jax.ops.segment_sum(src, seg, n)
kernel_name = 'mk_cond_resid_d4_seqx_r2_c8251d'

def setup_inputs(seed: int=0):
    np.random.seed(seed)
    _w = jnp.asarray

    def _rec_inputs():
        import jax
        import jax.numpy as jnp
        _rk = jax.random.key(seed)
        x = -0.0003929 + 0.9999 * jax.random.normal(jax.random.fold_in(_rk, 1), (128, 128, 512), jnp.float32)
        _lenS = 128 - jax.random.randint(jax.random.fold_in(_rk, 7), (128,), 0, max(1, 128 // 4) + 1, jnp.int32)
        _lenS2 = 128 - jax.random.randint(jax.random.fold_in(_rk, 8), (128,), 0, max(1, 128 // 4) + 1, jnp.int32)
        itok_B_0_2 = jax.random.randint(jax.random.fold_in(_rk, 11), (128,), 0, 3, jnp.int32)
        itok_B_0_8 = jax.random.randint(jax.random.fold_in(_rk, 12), (128,), 0, 9, jnp.int32)
        condB_zX = jax.random.uniform(jax.random.fold_in(_rk, 13), (128,), jnp.float32, 0.0, 0.983423)
        condB_zY = jax.random.uniform(jax.random.fold_in(_rk, 14), (128,), jnp.float32, 0.0, 0.979075)
        condB_zR = jax.random.uniform(jax.random.fold_in(_rk, 15), (128,), jnp.float32, 0.0, 0.9968)
        itok_B_0_63 = jax.random.randint(jax.random.fold_in(_rk, 16), (128,), 0, 64, jnp.int32)
        return (x, itok_B_0_2, itok_B_0_8, condB_zX, condB_zY, condB_zR, itok_B_0_63)
    x, itok_B_0_2, itok_B_0_8, condB_zX, condB_zY, condB_zR, itok_B_0_63 = _rec_inputs()

    def _L0_cond_setup():
        import jax, jax.numpy as jnp
        import numpy as np
        NEG_INF = -1e+30
        key = jax.random.key(seed)
        k1, k2, k3, k4, k5 = jax.random.split(key, 5)
        B, S, D, A = (16, 512, 512, 128)
        hidden = jax.random.normal(k1, (B, S, D), dtype=jnp.float32)
        W1 = jax.random.normal(k2, (D, A), dtype=jnp.float32) / np.sqrt(D)
        b1 = jax.random.normal(k3, (A,), dtype=jnp.float32) * 0.01
        v = jax.random.normal(k4, (A,), dtype=jnp.float32) / np.sqrt(A)
        prompt_type_ids = jax.random.randint(k5, (B,), 0, 3, dtype=jnp.int32)
        return {'hidden': hidden, 'W1': W1, 'b1': b1, 'v': v, 'prompt_type_ids': prompt_type_ids}
    _L0_cond_all = _L0_cond_setup()
    _L0_cond_in = {k: v for k, v in _L0_cond_all.items() if k in ('W1', 'b1', 'v')}
    del _L0_cond_all

    def _L1_cond_setup():
        import jax, jax.numpy as jnp
        import numpy as np
        LN_EPS = 1e-05
        key = jax.random.key(seed)
        ks = jax.random.split(key, 8)
        B, S, H, A, L = (32, 1024, 512, 128, 10)
        return {'hidden_states': jax.random.normal(ks[0], (B, S, H), dtype=jnp.float32), 'language_ids': jax.random.randint(ks[1], (B,), 0, L, dtype=jnp.int64), 'W1': jax.random.normal(ks[2], (L, H, A), dtype=jnp.float32) * (1.0 / np.sqrt(H)), 'b1': jnp.zeros((L, A), dtype=jnp.float32), 'W2': jax.random.normal(ks[3], (L, A, H), dtype=jnp.float32) * (1.0 / np.sqrt(A)), 'b2': jnp.zeros((L, H), dtype=jnp.float32), 'gamma': jnp.ones((L, H), dtype=jnp.float32), 'beta': jnp.zeros((L, H), dtype=jnp.float32)}
    _L1_cond_all = _L1_cond_setup()
    _L1_cond_in = {k: v for k, v in _L1_cond_all.items() if k in ('W1', 'b1', 'W2', 'b2', 'gamma', 'beta')}
    del _L1_cond_all

    def _L2_cond_setup():
        import jax, jax.numpy as jnp
        import numpy as np
        key = jax.random.key(seed)
        k1, k2, k3, k4 = jax.random.split(key, 4)
        B, H, W = (64, 512, 512)
        return {'y': jax.random.uniform(k1, (B, H, W), dtype=jnp.float32), 'zX': jax.random.uniform(k2, (B, 1), dtype=jnp.float32), 'zY': jax.random.uniform(k3, (B, 1), dtype=jnp.float32), 'zR': jax.random.uniform(k4, (B, 1), dtype=jnp.float32), 'dx': 1, 'dy': 1}
    _L2_cond_all = _L2_cond_setup()
    _L2_cond_in = {k: v for k, v in _L2_cond_all.items() if k in ()}
    del _L2_cond_all

    def _L3_cond_setup():
        import jax, jax.numpy as jnp
        import numpy as np
        NUM_CATEGORIES = 64
        INPUT_DIM = 512
        HIDDEN_DIM = 512
        B = 128
        S = 64
        key = jax.random.key(seed)
        kx, kc, kw = jax.random.split(key, 3)
        x = jax.random.normal(kx, (B, S, INPUT_DIM), dtype=jnp.float32)
        cat_ids = jax.random.randint(kc, (B,), 0, NUM_CATEGORIES, dtype=jnp.int32)
        W = 0.02 * jax.random.normal(kw, (NUM_CATEGORIES, INPUT_DIM, HIDDEN_DIM), dtype=jnp.float32)
        b = jnp.zeros((NUM_CATEGORIES, HIDDEN_DIM), dtype=jnp.float32)
        return {'x': x, 'cat_ids': cat_ids, 'W': W, 'b': b}
    _L3_cond_all = _L3_cond_setup()
    _L3_cond_in = {k: v for k, v in _L3_cond_all.items() if k in ('W', 'b')}
    del _L3_cond_all
    return {'x': x, 'itok_B_0_2': itok_B_0_2, 'itok_B_0_8': itok_B_0_8, 'condB_zX': condB_zX, 'condB_zY': condB_zY, 'condB_zR': condB_zR, 'itok_B_0_63': itok_B_0_63, 'L0_cond_W1': _L0_cond_in['W1'], 'L0_cond_b1': _L0_cond_in['b1'], 'L0_cond_v': _L0_cond_in['v'], 'L1_cond_W1': _L1_cond_in['W1'], 'L1_cond_b1': _L1_cond_in['b1'], 'L1_cond_W2': _L1_cond_in['W2'], 'L1_cond_b2': _L1_cond_in['b2'], 'L1_cond_gamma': _L1_cond_in['gamma'], 'L1_cond_beta': _L1_cond_in['beta'], 'L3_cond_W': _L3_cond_in['W'], 'L3_cond_b': _L3_cond_in['b']}

def reference(x, itok_B_0_2, itok_B_0_8, condB_zX, condB_zY, condB_zR, itok_B_0_63, L0_cond_W1, L0_cond_b1, L0_cond_v, L1_cond_W1, L1_cond_b1, L1_cond_W2, L1_cond_b2, L1_cond_gamma, L1_cond_beta, L3_cond_W, L3_cond_b):
    import jax
    import jax.numpy as jnp

    def _L0_cond_ref(hidden, W1, b1, v, prompt_type_ids):
        import jax, jax.numpy as jnp
        import numpy as np
        NEG_INF = -1e+30
        B, S, D = hidden.shape
        attn_in = jnp.tanh(jnp.einsum('bsd,da->bsa', hidden, W1) + b1)
        scores = jnp.einsum('bsa,a->bs', attn_in, v)
        idx = jnp.arange(S)
        j = idx[:, None]
        l = idx[None, :]
        prefix_m = l <= j
        postfix_m = l >= j
        cloze_m = l != j
        pt = prompt_type_ids[:, None, None]
        mask = jnp.where(pt == 0, prefix_m[None], jnp.where(pt == 1, postfix_m[None], cloze_m[None]))
        masked_scores = jnp.where(mask, scores[:, None, :], NEG_INF)
        p = jax.nn.softmax(masked_scores, axis=-1)
        cnt = jnp.sum(mask, axis=-1).astype(hidden.dtype)
        pooled = jnp.einsum('bjl,bld->bjd', p, hidden) / cnt[..., None]
        return pooled

    def _L1_cond_ref(hidden_states, language_ids, W1, b1, W2, b2, gamma, beta):
        import jax, jax.numpy as jnp
        import numpy as np
        LN_EPS = 1e-05
        w1 = W1[language_ids]
        w2 = W2[language_ids]
        h = jnp.einsum('bsh,bha->bsa', hidden_states, w1) + b1[language_ids][:, None, :]
        h = jax.nn.relu(h)
        adapted = jnp.einsum('bsa,bah->bsh', h, w2) + b2[language_ids][:, None, :]
        x = hidden_states + adapted
        mean = jnp.mean(x, axis=-1, keepdims=True)
        var = jnp.mean(jnp.square(x - mean), axis=-1, keepdims=True)
        normed = (x - mean) * jax.lax.rsqrt(var + LN_EPS)
        return normed * gamma[language_ids][:, None, :] + beta[language_ids][:, None, :]

    def _L2_cond_ref(y, zX, zY, zR, dx, dy):
        import jax, jax.numpy as jnp
        import numpy as np
        yp_x = jnp.pad(y, ((0, 0), (0, 0), (1, 1)), mode='reflect')
        lap_x = (yp_x[:, :, :-2] - 2.0 * y + yp_x[:, :, 2:]) / (dx * dx)
        yp_y = jnp.pad(y, ((0, 0), (1, 1), (0, 0)), mode='reflect')
        lap_y = (yp_y[:, :-2, :] - 2.0 * y + yp_y[:, 2:, :]) / (dy * dy)
        du_dt = zX[:, :, None] * lap_x + zY[:, :, None] * lap_y + zR[:, :, None] * y * (1.0 - y)
        return du_dt

    def _L3_cond_ref(x, cat_ids, W, b):
        import jax, jax.numpy as jnp
        import numpy as np
        NUM_CATEGORIES = 64
        INPUT_DIM = 512
        HIDDEN_DIM = 512
        B = 128
        S = 64
        selected_W = W[cat_ids]
        selected_b = b[cat_ids]
        out = jnp.einsum('bsd,bdh->bsh', x, selected_W) + selected_b[:, None, :]
        return out
    x = x + _L0_cond_ref(x, L0_cond_W1, L0_cond_b1, L0_cond_v, itok_B_0_2)
    x = x + _L1_cond_ref(x, itok_B_0_8, L1_cond_W1, L1_cond_b1, L1_cond_W2, L1_cond_b2, L1_cond_gamma, L1_cond_beta)
    x = x + _L2_cond_ref(x, condB_zX[:, None], condB_zY[:, None], condB_zR[:, None], 1, 1)
    x = x + _L3_cond_ref(x, itok_B_0_63, L3_cond_W, L3_cond_b)
    return x

_drawn_inputs = setup_inputs


def setup_inputs(seed=0):
    import zlib

    import numpy as np

    out = dict(_drawn_inputs(seed))
    spreads = {'L1_cond_b1': (0.0, 0.1),
     'L1_cond_b2': (0.0, 0.1),
     'L1_cond_gamma': (1.0, 0.2),
     'L1_cond_beta': (0.0, 0.1),
     'L3_cond_b': (0.0, 0.431)}
    factors = {'L0_cond_W1': 4.154, 'L0_cond_b1': 8.0, 'L0_cond_v': 3.554}
    for name, (base, spread) in spreads.items():
        noise = np.random.default_rng([zlib.crc32(name.encode()), seed]).standard_normal(out[name].shape)
        drawn = base * np.exp(spread * noise) if base else spread * noise
        out[name] = jnp.asarray(drawn.astype(out[name].dtype))
    for name, factor in factors.items():
        out[name] = (out[name] * factor).astype(out[name].dtype)
    return out
```

```python
import numpy as np
import concourse.bass as bass
from concourse import mybir
from contextlib import ExitStack

F32 = mybir.dt.float32
BF16 = mybir.dt.bfloat16
I32 = mybir.dt.int32
ALU = mybir.AluOpType
ACT = mybir.ActivationFunctionType
AX = mybir.AxisListType

P = 128
NEG = -1e30
EPS = 1e-5
UNROLL = 4
ITEM, CAT, LANG, KIND, FRESH, WSLOT, NPARAM = 0, 1, 2, 3, 4, 5, 8


class Step:

    def __init__(self, first, turn):
        self.first, self.turn = first, turn

    def __add__(self, k):
        return Step(self.first + k, self.turn)

    def __sub__(self, k):
        return self + (-k)

    @property
    def n(self):
        return self.first + self.turn * UNROLL

    def upto(self, back=0):
        return self.first + 1 - back + self.turn * UNROLL

    def dma(self):
        return 16 * (self.first // UNROLL + 1) + self.turn * 16

    def ring(self, size):
        return self.first % size

    def is_at_least(self, k):
        return self.first >= k


def run_slots(eng, body, first, last, steady_first, steady_last):
    turns = (steady_last - steady_first + 1) // UNROLL
    for s in range(first, steady_first):
        body(Step(s, 0))
    with eng.Fori(0, turns) as turn:
        for j in range(UNROLL):
            body(Step(steady_first + j, turn))
    for s in range(steady_first + turns * UNROLL, last + 1):
        body(Step(s, 0))


def cond_residual_kernel(nc, x, xT, kinds, langs, zx, zy, zr, cats, w1a, b1a, va,
                         w1l, b1l, w2l, b2l, gamma, beta, w3, b3, out):
    B, S, D = x.shape
    A = w1a.shape[1] // (D // P)
    K = D // P
    L = gamma.shape[0]
    C = w3.shape[0]
    ctx = ExitStack()

    def sb(name, shape, dt=F32):
        return ctx.enter_context(nc.sbuf_tensor(name, shape, dt))

    def pb(name):
        return ctx.enter_context(nc.psum_tensor(name, [P, 512], F32))

    def sem(name):
        return ctx.enter_context(nc.semaphore(name))

    def ring_sems(name, size=UNROLL):
        return [sem(f"{name}{i}") for i in range(size)]

    with ctx:
        b3_parts_dram = nc.dram_tensor("b3_parts_dram", [C, 3, D], BF16, kind="Internal").ap()

        w1_attn = sb("w1_attn", [P, K * A])
        b1_attn = sb("b1_attn", [P, 1])
        v_col = sb("v_col", [P, 1])
        v_wide = sb("v_wide", [P, P])
        w2_all = sb("w2_all", [P, L * D])
        b1_all = sb("b1_all", [P, L])
        b2_wide = sb("b2_wide", [P, L * D])
        gamma_wide = sb("gamma_wide", [P, L * D])
        beta_wide = sb("beta_wide", [P, L * D])
        ident = sb("ident", [P, P])
        ident16 = sb("ident16", [P, P], BF16)
        masks16 = sb("masks16", [P, 3 * P], BF16)
        rows_shift = sb("rows_shift", [P, P])
        ones3 = sb("ones3", [3, P], BF16)
        iota_row = sb("iota_row", [P, P])
        iota_col = sb("iota_col", [P, 1])
        minus_half = sb("minus_half", [P, 1])
        pool_mark = sb("pool_mark", [P, 1])
        dve_mark = sb("dve_mark", [P, 1])
        ones2 = sb("ones2", [P, 2])
        count_t = sb("count_t", [P, B])
        zx_t = sb("zx_t", [P, B])
        zy_t = sb("zy_t", [P, B])
        nzr_t = sb("nzr_t", [P, B])
        c0_t = sb("c0_t", [P, B])
        kind_t = sb("kind_t", [P, B])
        params_by_item = sb("params_by_item", [P, NPARAM], I32)
        params = sb("params", [1, B * NPARAM], I32)
        ids_col = sb("ids_col", [P, 3], I32)
        cat_row_i = sb("cat_row_i", [P, B], I32)
        vals = sb("vals", [P, 12])
        rank_col = sb("rank_col", [P, 1])
        key_col = sb("key_col", [P, 1])
        seen_col = sb("seen_col", [P, 1])
        fresh_col = sb("fresh_col", [P, 1])
        slot_i = sb("slot_i", [P, 2], I32)

        xs = sb("xs", [P, 4, D])
        xts = sb("xts", [P, 4, K, S])
        w1s = sb("w1s", [P, 4, K, A])
        w3s = sb("w3s", [P, 4 * K * D])
        b3s = sb("b3s", [3, 4, D], BF16)
        cat_row, key_row, less, same, place, tmp = (w3s[:, i * P:(i + 1) * P] for i in range(6))
        wide = w3s[:, 6 * P:10 * P]
        b3_f, b3_rest = w3s[0:C, 10 * P:10 * P + D], w3s[0:C, 10 * P + D:10 * P + 2 * D]
        b3_parts = w3s[0:C, 10 * P + 2 * D:10 * P + 4 * D].bitcast(BF16)
        attn = sb("attn", [P, 2, S])
        neg_max = sb("neg_max", [P, 2])
        probs = sb("probs", [P, 2, S])
        prob_sum = sb("prob_sum", [P, 2])
        denom = sb("denom", [P, 2])
        scale = sb("scale", [P, 2])
        probsT = sb("probsT", [P, 2, S])
        x1 = sb("x1", [P, 2, D])
        x1T = sb("x1T", [P, 2, D])
        x1_b2 = sb("x1_b2", [P, 2, D])
        x1_beta = sb("x1_beta", [P, 2, D])
        hid = sb("hid", [P, 2, S])
        y = sb("y", [P, 2, D])
        y_sum = sb("y_sum", [P, 2])
        neg_mean = sb("neg_mean", [P, 2])
        square_junk = sb("square_junk", [P, D])
        var_sum = sb("var_sum", [P, 2])
        var_eps = sb("var_eps", [P, 2])
        rstd = sb("rstd", [P, 2])
        x2 = sb("x2", [P, 2, D + 2])
        react = sb("react", [P, 2, D])
        neighbours = sb("neighbours", [P, 2, D])
        rows_mix = sb("rows_mix", [P, 2, P])
        x3 = sb("x3", [P, 4, D])
        x3T = sb("x3T", [P, 2, D])
        res = sb("res", [P, 4, D])

        bank_small = pb("bank_small")
        ps_attn, ps_probsT = bank_small[:, 0:S], bank_small[:, S:2 * S]
        bank_scores = pb("bank_scores")
        ps_scores = bank_scores[:, 0:S]
        ps_pool = pb("ps_pool")
        ps_T = pb("ps_T")
        bank_hid = pb("bank_hid")
        ps_hid = bank_hid[:, 0:S]
        ps_adapt = pb("ps_adapt")
        ps_rows = pb("ps_rows")
        ps_out = pb("ps_out")

        tables_in = sem("tables_in")
        ids_in = sem("ids_in")
        b3_in = sem("b3_in")
        b3_parts_out = sem("b3_parts_out")
        params_in = sem("params_in")
        x_in, xT_in, w1_in = ring_sems("x_in"), ring_sems("xT_in"), ring_sems("w1_in")
        w3_in, b3row_in, res_out = ring_sems("w3_in"), ring_sems("b3row_in"), ring_sems("res_out")
        consts_made = sem("consts_made")
        prep = sem("prep")
        pool_prep = sem("pool_prep")
        b3_split = sem("b3_split")
        fresh_made, slots_summed = sem("fresh_made"), sem("slots_summed")
        place_made, sorted_made, tables_made = sem("place_made"), sem("sorted_made"), sem("tables_made")
        params_made = sem("params_made")
        gconst = sem("gconst")
        attn_mm, scores_mm, probsT_mm, pool_mm = (sem(n) for n in ("attn_mm", "scores_mm", "probsT_mm", "pool_mm"))
        x1T_mm, hid_mm, adapt_mm, rows_mm, x3T_mm, out_mm = (
            sem(n) for n in ("x1T_mm", "hid_mm", "adapt_mm", "rows_mm", "x3T_mm", "out_mm"))
        attn_ready, probs_ready, probsT_ready, x1T_ready, var_ready, react_ready, x3T_ready = (
            sem(n) for n in ("attn_ready", "probs_ready", "probsT_ready", "x1T_ready", "var_ready",
                             "react_ready", "x3T_ready"))
        max_ready, denom_ready, scale_ready, x1_ready, hid_ready, y_ready, mean_ready, norm_ready = (
            sem(n) for n in ("max_ready", "denom_ready", "scale_ready", "x1_ready", "hid_ready", "y_ready",
                             "mean_ready", "norm_ready"))
        x2_ready, partial_ready, x3_ready, res_ready = (
            sem(n) for n in ("x2_ready", "partial_ready", "x3_ready", "res_ready"))
        edges_ready, neighbours_ready, react_x2_ready, x1_b2_ready, x1_beta_ready, rows_mix_ready = (
            sem(n) for n in ("edges_ready", "neighbours_ready", "react_x2_ready", "x1_b2_ready",
                             "x1_beta_ready", "rows_mix_ready"))
        vareps_ready, rstd_ready = sem("vareps_ready"), sem("rstd_ready")

        block = ctx.enter_context(nc.Block())

        def param(eng, item, what, top):
            return eng.value_load(params[0:1, bass.ds(item.n * NPARAM + what, 1)], min_val=0, max_val=top)

        @block.sync
        def _(sp):
            sp.dma_start(ids_col[:, 0:1], cats).then_inc(ids_in, 16)
            sp.dma_start(ids_col[:, 1:2], langs).then_inc(ids_in, 16)
            sp.dma_start(ids_col[:, 2:3], kinds).then_inc(ids_in, 16)
            sp.dma_start(vals[:, 4:5], zx).then_inc(ids_in, 16)
            sp.dma_start(vals[:, 5:6], zy).then_inc(ids_in, 16)
            sp.dma_start(vals[:, 6:7], zr).then_inc(ids_in, 16)
            sp.dma_start(cat_row_i[:, :], cats.rearrange("b o -> (o b)").partition_broadcast(P)).then_inc(ids_in, 16)
            sp.dma_start(v_col[:, :], va).then_inc(ids_in, 16)
            sp.dma_start(b3_f[:, :], b3).then_inc(b3_in, 16)
            sp.dma_start(w1_attn[:, :], w1a).then_inc(tables_in, 16)
            sp.dma_start(b1_attn[:, :], b1a).then_inc(tables_in, 16)
            sp.dma_start(b1_all[:, :], b1l).then_inc(tables_in, 16)
            sp.dma_start(w2_all[:, :], w2l).then_inc(tables_in, 16)
            for table, src in ((b2_wide, b2l), (gamma_wide, gamma), (beta_wide, beta)):
                sp.dma_start(table[:, :], src.rearrange("l d -> (l d)").partition_broadcast(P)).then_inc(tables_in, 16)
            sp.wait_ge(b3_split, 1)
            sp.dma_start(b3_parts_dram, b3_parts[:, 0:3 * D].rearrange("c (t d) -> c t d", t=3)).then_inc(b3_parts_out, 16)
            sp.wait_ge(params_made, 1)
            sp.dma_start(params[0:1, :], params_by_item[:, :]).then_inc(params_in, 16)
            sp.wait_ge(params_in, 16)
            sp.wait_ge(b3_parts_out, 16)
            sp.wait_ge(tables_made, 1)

            def slot(s):
                a = s + 3
                if s.first + 3 < B or s.turn is not 0:
                    item = param(sp, a, ITEM, B - 1)
                    lang = param(sp, a, LANG, L - 1)
                    r = a.ring(4)
                    if a.is_at_least(4):
                        sp.wait_ge(attn_mm, a.upto(4))
                    sp.dma_start(xts[:, r], xT[bass.ds(item, 1)].rearrange("o p (k s) -> p (o k) s", k=K)
                                 ).then_inc(xT_in[r], 16)
                    if a.is_at_least(4):
                        sp.wait_ge(x1_ready, a.upto(4))
                    sp.dma_start(xs[:, r], x[bass.ds(item, 1)].rearrange("o s d -> s (o d)")).then_inc(x_in[r], 16)
                    if a.is_at_least(4):
                        sp.wait_ge(hid_mm, a.upto(4))
                    sp.dma_start(w1s[:, r], w1l[bass.ds(lang, 1)].rearrange("o p (k a) -> p (o k) a", k=K)
                                 ).then_inc(w1_in[r], 16)
                c = s + 1
                if (s.first + 1 >= 0 and s.first + 1 < B) or s.turn is not 0:
                    cat = param(sp, c, CAT, C - 1)
                    fresh = param(sp, c, FRESH, 1)
                    wslot = param(sp, c, WSLOT, 3)
                    r = c.ring(4)
                    if c.is_at_least(4):
                        sp.wait_ge(out_mm, c.upto(4))
                    sp.dma_start(w3s[:, bass.ds(wslot * (K * D), K * D)],
                                 w3[bass.ds(cat, 1)].rearrange("o p n -> p (o n)"),
                                 cond=fresh, bounds_check="skip_entire_dma").then_inc(w3_in[r], 16)
                    sp.dma_start(b3s[:, r], b3_parts_dram[bass.ds(cat, 1)].rearrange("o t d -> t (o d)")
                                 ).then_inc(b3row_in[r], 16)
                o = s - 3
                if s.first - 3 >= 0:
                    item = param(sp, o, ITEM, B - 1)
                    r = o.ring(4)
                    sp.wait_ge(res_ready, o.upto())
                    sp.dma_start(out[bass.ds(item, 1)].rearrange("o s d -> s (o d)"), res[:, r]
                                 ).then_inc(res_out[r], 16)

            run_slots(sp, slot, -3, B + 2, 5, B - 4)
            for r in range(4):
                sp.wait_ge(res_out[r], 16 * (B // 4))

        @block.tensor
        def _(pe):
            pe.wait_ge(fresh_made, 1)
            pe.matmul(ps_pool[:, 0:1], less[:, :], fresh_col[:, :], start=True, stop=True).then_inc(slots_summed, 1)
            pe.wait_ge(place_made, 1)
            pe.matmul(ps_adapt[:, 0:NPARAM], place[:, :], vals[:, 0:NPARAM], start=True, stop=True
                      ).then_inc(sorted_made, 1)
            for i in range(4):
                mm = pe.matmul(ps_rows[:, i * P:(i + 1) * P], wide[:, i * P:(i + 1) * P], place[:, :],
                               start=True, stop=True)
            mm.then_inc(sorted_made, 1)
            pe.wait_ge(tables_made, 1)
            pe.wait_ge(gconst, 1)
            pe.wait_ge(tables_in, 16 * 7)
            pe.wait_ge(params_in, 16)

            def attn_project(a):
                r = a.ring(4)
                pe.wait_ge(xT_in[r], a.dma())
                if a.is_at_least(1):
                    pe.wait_ge(attn_ready, a.upto(1))
                if a.is_at_least(2):
                    pe.wait_ge(probsT_ready, a.upto(2))
                for k in range(K):
                    mm = pe.matmul(ps_attn, w1_attn[:, k * A:(k + 1) * A], xts[:, r, k, :],
                                   start=(k == 0), stop=(k == K - 1))
                mm.then_inc(attn_mm, 1)

            def attn_scores(b):
                kind = param(pe, b, KIND, 2)
                pe.wait_ge(attn_ready, b.upto())
                if b.is_at_least(1):
                    pe.wait_ge(probs_ready, b.upto(1))
                pe.matmul(ps_scores, v_wide[:, :], attn[:, b.ring(2), :], start=True, stop=False)
                pe.matmul(ps_scores, ident16[:, :], masks16[:, bass.ds(kind * P, P)], start=False, stop=True
                          ).then_inc(scores_mm, 1)

            def probs_transpose(c):
                pe.wait_ge(probs_ready, c.upto())
                if c.first + 1 < B or c.turn is not 0:
                    pe.wait_ge(attn_ready, (c + 1).upto())
                pe.transpose(ps_probsT, probs[:, c.ring(2), :], ident[:, :]).then_inc(probsT_mm, 1)

            def pool(d):
                pe.wait_ge(probsT_ready, d.upto())
                pe.wait_ge(x_in[d.ring(4)], d.dma())
                if d.is_at_least(1):
                    pe.wait_ge(x1_ready, d.upto(1))
                pe.matmul(ps_pool[:, :], probsT[:, d.ring(2), :], xs[:, d.ring(4), :], start=True, stop=True
                          ).then_inc(pool_mm, 1)

            def x1_transpose(e):
                pe.wait_ge(x1_ready, e.upto())
                if e.is_at_least(2):
                    pe.wait_ge(x3T_ready, e.upto(2))
                for k in range(K):
                    mm = pe.transpose(ps_T[:, k * P:(k + 1) * P], x1[:, e.ring(2), k * P:(k + 1) * P], ident[:, :])
                mm.then_inc(x1T_mm, 1)

            def x3_transpose(i):
                pe.wait_ge(x3_ready, i.upto())
                if i.first + 1 < B or i.turn is not 0:
                    pe.wait_ge(x1T_ready, (i + 1).upto())
                for k in range(K):
                    mm = pe.transpose(ps_T[:, k * P:(k + 1) * P], x3[:, i.ring(4), k * P:(k + 1) * P], ident[:, :])
                mm.then_inc(x3T_mm, 1)

            def adapter_down(f):
                pe.wait_ge(x1T_ready, f.upto())
                pe.wait_ge(w1_in[f.ring(4)], f.dma())
                if f.is_at_least(1):
                    pe.wait_ge(hid_ready, f.upto(1))
                for k in range(K):
                    mm = pe.matmul(ps_hid, w1s[:, f.ring(4), k, :], x1T[:, f.ring(2), k * P:(k + 1) * P],
                                   start=(k == 0), stop=(k == K - 1))
                mm.then_inc(hid_mm, 1)

            def adapter_up(g):
                lang = param(pe, g, LANG, L - 1)
                pe.wait_ge(hid_ready, g.upto())
                if g.is_at_least(1):
                    pe.wait_ge(y_ready, g.upto(1))
                pe.matmul(ps_adapt[:, :], hid[:, g.ring(2), :], w2_all[:, bass.ds(lang * D, D)],
                          start=True, stop=True).then_inc(adapt_mm, 1)

            def rows_laplacian(h):
                pe.wait_ge(x2_ready, h.upto())
                pe.wait_ge(rows_mix_ready, h.upto())
                if h.is_at_least(1):
                    pe.wait_ge(partial_ready, h.upto(1))
                pe.matmul(ps_rows[:, :], rows_mix[:, h.ring(2), :], x2[:, h.ring(2), 1:D + 1],
                          start=True, stop=True).then_inc(rows_mm, 1)

            def category_first(j):
                wslot = param(pe, j, WSLOT, 3)
                pe.wait_ge(x3T_ready, j.upto())
                pe.wait_ge(w3_in[j.ring(4)], j.dma())
                pe.wait_ge(b3row_in[j.ring(4)], j.dma())
                if j.is_at_least(1):
                    pe.wait_ge(res_ready, j.upto(1))
                for k in range(2):
                    pe.matmul(ps_out[:, :], x3T[:, j.ring(2), k * P:(k + 1) * P],
                              w3s[:, bass.ds(wslot * (K * D) + k * D, D)], start=(k == 0), stop=False)
                return wslot

            def category_second(j, wslot):
                for k in range(2, K):
                    pe.matmul(ps_out[:, :], x3T[:, j.ring(2), k * P:(k + 1) * P],
                              w3s[:, bass.ds(wslot * (K * D) + k * D, D)], start=False, stop=False)
                pe.matmul(ps_out[:, :], ones3[:, :], b3s[:, j.ring(4), :], start=False, stop=True
                          ).then_inc(out_mm, 1)

            def inside(s, k):
                return s.turn is not 0 or 0 <= s.first + k < B

            def slot(s):
                if inside(s, -2):
                    x3_transpose(s - 2)
                if inside(s, 0):
                    pool(s)
                if inside(s, -2):
                    wslot = category_first(s - 2)
                if inside(s, 0):
                    x1_transpose(s)
                if inside(s, -1):
                    rows_laplacian(s - 1)
                if inside(s, 2):
                    attn_project(s + 2)
                if inside(s, 0):
                    adapter_down(s)
                if inside(s, 1):
                    attn_scores(s + 1)
                if inside(s, 0):
                    adapter_up(s)
                if inside(s, 1):
                    probs_transpose(s + 1)
                if inside(s, -2):
                    category_second(s - 2, wslot)

            run_slots(pe, slot, -2, B + 1, 6, B - 3)

        @block.scalar
        def _(act):
            act.wait_ge(tables_made, 1)
            act.wait_ge(tables_in, 16 * 7)

            def inside(s, k):
                return s.turn is not 0 or 0 <= s.first + k < B

            def slot(s):
                if inside(s, -2):
                    i = s - 2
                    act.wait_ge(x3T_mm, i.upto())
                    if i.is_at_least(2):
                        act.wait_ge(out_mm, i.upto(2))
                    nc.scalar.activation(x3T[:, i.ring(2), :], ps_T[:, :], ACT.Copy).then_inc(x3T_ready, 1)
                if inside(s, -1):
                    h = s - 1
                    act.wait_ge(x2_ready, h.upto())
                    if h.is_at_least(2):
                        act.wait_ge(partial_ready, h.upto(2))
                        act.wait_ge(x3_ready, h.upto(2))
                    nc.scalar.activation(react[:, h.ring(2), :], x2[:, h.ring(2), 1:D + 1], ACT.Identity,
                                         bias=c0_t[:, bass.ds(h.n, 1)], scale=nzr_t[:, bass.ds(h.n, 1)]
                                         ).then_inc(react_ready, 1)
                if inside(s, 0):
                    act.wait_ge(x1T_mm, s.upto())
                    if s.is_at_least(2):
                        act.wait_ge(hid_mm, s.upto(2))
                    nc.scalar.activation(x1T[:, s.ring(2), :], ps_T[:, :], ACT.Copy).then_inc(x1T_ready, 1)
                if inside(s, 2):
                    a = s + 2
                    act.wait_ge(attn_mm, a.upto())
                    if a.is_at_least(2):
                        act.wait_ge(scores_mm, a.upto(2))
                    nc.scalar.activation(attn[:, a.ring(2), :], ps_attn, ACT.Tanh, bias=b1_attn[:, 0:1]
                                         ).then_inc(attn_ready, 1)
                if inside(s, 1):
                    b = s + 1
                    act.wait_ge(max_ready, b.upto())
                    if b.is_at_least(2):
                        act.wait_ge(probsT_mm, b.upto(2))
                        act.wait_ge(denom_ready, b.upto(2))
                    nc.scalar.activation(probs[:, b.ring(2), :], ps_scores, ACT.Exp,
                                         bias=neg_max[:, b.ring(2):b.ring(2) + 1],
                                         accum_out=prob_sum[:, b.ring(2):b.ring(2) + 1]).then_inc(probs_ready, 1)
                    act.wait_ge(probsT_mm, b.upto())
                    if b.is_at_least(2):
                        act.wait_ge(pool_mm, b.upto(2))
                    nc.scalar.activation(probsT[:, b.ring(2), :], ps_probsT, ACT.Copy).then_inc(probsT_ready, 1)
                if inside(s, 0):
                    act.wait_ge(mean_ready, s.upto())
                    if s.is_at_least(2):
                        act.wait_ge(vareps_ready, s.upto(2))
                    q = s.ring(2)
                    nc.scalar.activation(square_junk[:, :], y[:, q, :], ACT.Square, bias=neg_mean[:, q:q + 1],
                                         accum_out=var_sum[:, q:q + 1]).then_inc(var_ready, 1)

            run_slots(act, slot, -2, B + 1, 6, B - 3)

        @block.vector
        def _(dve):
            steps = [0]

            def then(ins):
                steps[0] += 1
                ins.then_inc(prep, 1)
                dve.wait_ge(prep, steps[0])

            dve.wait_ge(ids_in, 16 * 8)
            dve.wait_ge(consts_made, 1)
            nc.vector.memset(ones3[:, :], 1.0)
            nc.vector.memset(minus_half[:, :], -0.5)
            nc.vector.memset(ones2[:, :], 1.0)
            nc.vector.tensor_copy(vals[:, 0:1], iota_col[:, :])
            nc.vector.tensor_copy(vals[:, 1:4], ids_col[:, :])
            nc.vector.tensor_copy(ident16[:, :], ident[:, :])
            then(nc.vector.tensor_copy(cat_row[:, :], cat_row_i[:, :]))
            nc.vector.scalar_tensor_tensor(key_row[:, :], cat_row[:, :], float(B), iota_row[:, :], ALU.mult, ALU.add)
            then(nc.vector.scalar_tensor_tensor(key_col[:, :], vals[:, 1:2], float(B), iota_col[:, :], ALU.mult, ALU.add))
            then(nc.vector.tensor_scalar(less[:, :], key_row[:, :], key_col[:, 0:1], None, ALU.is_lt))
            nc.vector.tensor_reduce(rank_col[:, :], less[:, :], AX.X, ALU.add)
            then(nc.vector.tensor_scalar(same[:, :], cat_row[:, :], vals[:, 1:2], None, ALU.is_equal))
            then(nc.vector.tensor_tensor(same[:, :], same[:, :], less[:, :], ALU.mult))
            then(nc.vector.tensor_reduce(seen_col[:, :], same[:, :], AX.X, ALU.add))
            nc.vector.tensor_scalar(fresh_col[:, :], seen_col[:, :], 0.0, None, ALU.is_equal)
            then(nc.vector.tensor_scalar(less[:, :], cat_row[:, :], vals[:, 1:2], None, ALU.is_gt))
            nc.vector.tensor_copy(vals[:, 7:8], vals[:, 4:5])
            nc.vector.tensor_copy(vals[:, 8:9], vals[:, 5:6])
            then(nc.vector.tensor_copy(vals[:, 9:10], vals[:, 6:7]))
            nc.vector.tensor_scalar(wide[:, 0:P], ident[:, :], 0.0, vals[:, 7:8], ALU.mult, ALU.add)
            nc.vector.tensor_scalar(wide[:, P:2 * P], ident[:, :], 0.0, vals[:, 8:9], ALU.mult, ALU.add)
            nc.vector.tensor_scalar(wide[:, 2 * P:3 * P], ident[:, :], 0.0, vals[:, 9:10], ALU.mult, ALU.add)
            nc.vector.tensor_scalar(wide[:, 3 * P:4 * P], ident[:, :], 0.0, vals[:, 3:4], ALU.mult, ALU.add)
            nc.vector.tensor_scalar(v_wide[:, :], ident[:, :], 0.0, v_col[:, 0:1], ALU.mult, ALU.add)
            nc.vector.tensor_copy(vals[:, FRESH:FRESH + 1], fresh_col[:, :]).then_inc(fresh_made, 1)
            dve.wait_ge(slots_summed, 1)
            then(nc.vector.tensor_copy(slot_i[:, 0:1], ps_pool[:, 0:1]))
            then(nc.vector.tensor_scalar(slot_i[:, 1:2], slot_i[:, 0:1], 3, None, ALU.bitwise_and))
            nc.vector.tensor_copy(vals[:, WSLOT:WSLOT + 1], slot_i[:, 1:2])
            nc.vector.memset(vals[:, 6:8], 0.0)
            nc.vector.tensor_scalar(place[:, :], iota_row[:, :], rank_col[:, 0:1], None, ALU.is_equal
                                    ).then_inc(place_made, 1)
            dve.wait_ge(sorted_made, 1)
            nc.vector.tensor_copy(params_by_item[:, :], ps_adapt[:, 0:NPARAM]).then_inc(params_made, 1)
            dve.wait_ge(sorted_made, 2)
            nc.vector.tensor_copy(zx_t[:, :], ps_rows[:, 0:P])
            nc.vector.tensor_copy(zy_t[:, :], ps_rows[:, P:2 * P])
            nc.vector.tensor_scalar(nzr_t[:, :], ps_rows[:, 2 * P:3 * P], -1.0, None, ALU.mult)
            then(nc.vector.tensor_copy(kind_t[:, :], ps_rows[:, 3 * P:4 * P]))
            then(nc.vector.tensor_tensor(tmp[:, :], zx_t[:, :], zy_t[:, :], ALU.add))
            then(nc.vector.tensor_scalar(tmp[:, :], tmp[:, :], -2.0, 1.0, ALU.mult, ALU.add))
            then(nc.vector.tensor_tensor(c0_t[:, :], tmp[:, :], nzr_t[:, :], ALU.subtract))
            nc.vector.tensor_scalar(key_col[:, :], iota_col[:, :], 1.0, None, ALU.add)
            nc.vector.tensor_scalar(seen_col[:, :], iota_col[:, :], -1.0, float(S), ALU.mult, ALU.add)
            then(nc.vector.tensor_scalar(tmp[:, :], kind_t[:, :], 0.0, None, ALU.is_equal))
            then(nc.vector.tensor_scalar(count_t[:, :], tmp[:, :], key_col[:, 0:1], None, ALU.mult))
            then(nc.vector.tensor_scalar(tmp[:, :], kind_t[:, :], 1.0, None, ALU.is_equal))
            then(nc.vector.scalar_tensor_tensor(count_t[:, :], tmp[:, :], seen_col[:, 0:1], count_t[:, :],
                                                ALU.mult, ALU.add))
            then(nc.vector.tensor_scalar(tmp[:, :], kind_t[:, :], 1.5, float(S - 1), ALU.is_gt, ALU.mult))
            then(nc.vector.tensor_tensor(count_t[:, :], count_t[:, :], tmp[:, :], ALU.add))
            dve.wait_ge(b3_in, 16)
            then(nc.vector.tensor_copy(b3_parts[:, 0:D], b3_f[:, :]))
            then(nc.vector.tensor_tensor(b3_rest[:, :], b3_f[:, :], b3_parts[:, 0:D], ALU.subtract))
            then(nc.vector.tensor_copy(b3_parts[:, D:2 * D], b3_rest[:, :]))
            then(nc.vector.tensor_tensor(b3_rest[:, :], b3_rest[:, :], b3_parts[:, D:2 * D], ALU.subtract))
            nc.vector.tensor_copy(b3_parts[:, 2 * D:3 * D], b3_rest[:, :]).then_inc(b3_split, 1)
            dve.wait_ge(b3_split, 1)
            nc.vector.memset(dve_mark[:, :], 0.0).then_inc(tables_made, 1)
            dve.wait_ge(tables_in, 16 * 7)
            dve.wait_ge(params_in, 16)

            def inside(s, k):
                return s.turn is not 0 or 0 <= s.first + k < B

            def slot(s):
                if inside(s, -1):
                    h = s - 1
                    q = h.ring(2)
                    lang = param(dve, h, LANG, L - 1)
                    dve.wait_ge(var_ready, h.upto())
                    if h.is_at_least(2):
                        dve.wait_ge(rstd_ready, h.upto(2))
                    nc.vector.tensor_scalar(var_eps[:, q:q + 1], var_sum[:, q:q + 1], 1.0 / D, EPS,
                                            ALU.mult, ALU.add).then_inc(vareps_ready, 1)
                    nc.vector.scalar_tensor_tensor(y[:, q, :], y[:, q, :], neg_mean[:, q:q + 1],
                                                   gamma_wide[:, bass.ds(lang * D, D)], ALU.add, ALU.mult
                                                   ).then_inc(norm_ready, 1)
                if inside(s, -3):
                    o = s - 3
                    dve.wait_ge(out_mm, o.upto())
                    if o.is_at_least(4):
                        dve.wait_ge(res_out[o.ring(4)], (o - 4).dma())
                    nc.vector.tensor_tensor(res[:, o.ring(4), :], ps_out[:, :], x3[:, o.ring(4), :], ALU.add
                                            ).then_inc(res_ready, 1)
                if inside(s, -1):
                    dve.wait_ge(norm_ready, h.upto())
                    dve.wait_ge(rstd_ready, h.upto())
                    dve.wait_ge(x1_beta_ready, h.upto())
                    if h.is_at_least(2):
                        dve.wait_ge(rows_mm, h.upto(2))
                        dve.wait_ge(react_x2_ready, h.upto(2))
                        dve.wait_ge(neighbours_ready, h.upto(2))
                    nc.vector.scalar_tensor_tensor(x2[:, q, 1:D + 1], y[:, q, :], rstd[:, q:q + 1], x1_beta[:, q, :],
                                                   ALU.mult, ALU.add).then_inc(x2_ready, 1)
                if inside(s, 0):
                    q = s.ring(2)
                    dve.wait_ge(pool_mm, s.upto())
                    dve.wait_ge(scale_ready, s.upto())
                    if s.is_at_least(2):
                        dve.wait_ge(x1T_mm, s.upto(2))
                        dve.wait_ge(x1_beta_ready, s.upto(2))
                        dve.wait_ge(x1_b2_ready, s.upto(2))
                    nc.vector.scalar_tensor_tensor(x1[:, q, :], ps_pool[:, :], scale[:, q:q + 1], xs[:, s.ring(4), :],
                                                   ALU.mult, ALU.add).then_inc(x1_ready, 1)
                if inside(s, -1):
                    h = s - 1
                    q = h.ring(2)
                    dve.wait_ge(rows_mm, h.upto())
                    dve.wait_ge(react_x2_ready, h.upto())
                    nc.vector.tensor_tensor(react[:, q, :], ps_rows[:, :], react[:, q, :], ALU.add
                                            ).then_inc(partial_ready, 1)
                    dve.wait_ge(partial_ready, h.upto())
                    dve.wait_ge(neighbours_ready, h.upto())
                    if h.is_at_least(4):
                        dve.wait_ge(x3T_mm, h.upto(4))
                    nc.vector.scalar_tensor_tensor(x3[:, h.ring(4), :], neighbours[:, q, :], zx_t[:, bass.ds(h.n, 1)],
                                                   react[:, q, :], ALU.mult, ALU.add).then_inc(x3_ready, 1)
                if inside(s, 0):
                    lang = param(dve, s, LANG, L - 1)
                    dve.wait_ge(hid_mm, s.upto())
                    if s.is_at_least(2):
                        dve.wait_ge(adapt_mm, s.upto(2))
                    nc.vector.tensor_scalar(hid[:, s.ring(2), :], ps_hid, b1_all[:, bass.ds(lang, 1)], 0.0,
                                            ALU.add, ALU.max).then_inc(hid_ready, 1)
                if inside(s, 1):
                    b = s + 1
                    p = b.ring(2)
                    dve.wait_ge(scores_mm, b.upto())
                    if b.is_at_least(2):
                        dve.wait_ge(probs_ready, b.upto(2))
                    nc.vector.tensor_reduce(neg_max[:, p:p + 1], ps_scores, AX.X, ALU.max, negate=True
                                            ).then_inc(max_ready, 1)
                    dve.wait_ge(probs_ready, b.upto())
                    nc.vector.tensor_tensor(denom[:, p:p + 1], prob_sum[:, p:p + 1], count_t[:, bass.ds(b.n, 1)],
                                            ALU.mult).then_inc(denom_ready, 1)
                    dve.wait_ge(denom_ready, b.upto())
                    nc.vector.reciprocal(scale[:, p:p + 1], denom[:, p:p + 1]).then_inc(scale_ready, 1)
                if inside(s, 0):
                    q = s.ring(2)
                    dve.wait_ge(adapt_mm, s.upto())
                    dve.wait_ge(x1_b2_ready, s.upto())
                    nc.vector.scalar_tensor_tensor(y[:, q, :], ps_adapt[:, :], 1.0, x1_b2[:, q, :], ALU.mult, ALU.add,
                                                   accum_out=y_sum[:, q:q + 1]).then_inc(y_ready, 1)
                    dve.wait_ge(y_ready, s.upto())
                    nc.vector.tensor_scalar(neg_mean[:, q:q + 1], y_sum[:, q:q + 1], -1.0 / D, None, ALU.mult
                                            ).then_inc(mean_ready, 1)

            run_slots(dve, slot, -1, B + 2, 7, B - 2)

        @block.gpsimd
        def _(pool):
            steps = [0]

            def then(ins):
                steps[0] += 1
                ins.then_inc(pool_prep, 1)
                pool.wait_ge(pool_prep, steps[0])

            nc.gpsimd.memset(ident[:, :], 0.0)
            nc.gpsimd.memset(rows_shift[:, :], 0.0)
            nc.gpsimd.memset(masks16[:, :], 0.0)
            nc.gpsimd.iota(iota_row[:, :], [[1, P]], base=0, channel_multiplier=0,
                           allow_small_or_imprecise_dtypes=True)
            then(nc.gpsimd.iota(iota_col[:, :], [[0, 1]], base=0, channel_multiplier=1,
                                allow_small_or_imprecise_dtypes=True))

            nc.gpsimd.affine_select(ident[:, :], ident[:, :], [[-1, P]], ALU.not_equal, 1.0, base=0,
                                    channel_multiplier=1).then_inc(consts_made, 1)
            for base in (1, -1):
                then(nc.gpsimd.affine_select(rows_shift[:, :], rows_shift[:, :], [[-1, P]], ALU.not_equal, 1.0,
                                             base=base, channel_multiplier=1))
            for to, source in ((0, 1), (P - 1, P - 2)):
                then(nc.gpsimd.affine_select(rows_shift[:, to:to + 1], rows_shift[:, to:to + 1], [[0, 1]],
                                             ALU.not_equal, 2.0, base=-source, channel_multiplier=1))
            for m, (step, mult, op) in enumerate(((-1, 1, ALU.is_ge), (1, -1, ALU.is_ge), (-1, 1, ALU.not_equal))):
                then(nc.gpsimd.affine_select(masks16[:, m * P:(m + 1) * P], masks16[:, m * P:(m + 1) * P], [[step, P]],
                                             op, NEG, base=0, channel_multiplier=mult))
            nc.gpsimd.memset(pool_mark[:, :], 0.0).then_inc(gconst, 1)
            pool.wait_ge(tables_made, 1)
            pool.wait_ge(tables_in, 16 * 7)
            pool.wait_ge(params_in, 16)

            def inside(s, k):
                return s.turn is not 0 or 0 <= s.first + k < B

            def slot(s):
                if inside(s, -1):
                    h = s - 1
                    q = h.ring(2)
                    pool.wait_ge(vareps_ready, h.upto())
                    if h.is_at_least(2):
                        pool.wait_ge(x2_ready, h.upto(2))
                    nc.gpsimd.tensor_tensor(rstd[:, q:q + 1], var_eps[:, q:q + 1], minus_half[:, :], ALU.pow
                                            ).then_inc(rstd_ready, 1)
                    pool.wait_ge(x2_ready, h.upto())
                    ends = x2[:, q, 2:D:D - 3]
                    nc.gpsimd.tensor_tensor(x2[:, q, 0:D + 2:D + 1], ends, ones2[:, :], ALU.mult).then_inc(edges_ready, 1)
                    pool.wait_ge(edges_ready, h.upto())
                    if h.is_at_least(2):
                        pool.wait_ge(x3_ready, h.upto(2))
                    nc.gpsimd.tensor_tensor(neighbours[:, q, :], x2[:, q, 0:D], x2[:, q, 2:D + 2], ALU.add
                                            ).then_inc(neighbours_ready, 1)
                    pool.wait_ge(react_ready, h.upto())
                    if h.is_at_least(2):
                        pool.wait_ge(partial_ready, h.upto(2))
                    nc.gpsimd.tensor_tensor(react[:, q, :], react[:, q, :], x2[:, q, 1:D + 1], ALU.mult
                                            ).then_inc(react_x2_ready, 1)
                if inside(s, 0):
                    q = s.ring(2)
                    lang = param(pool, s, LANG, L - 1)
                    pool.wait_ge(x1_ready, s.upto())
                    if s.is_at_least(2):
                        pool.wait_ge(y_ready, s.upto(2))
                    nc.gpsimd.tensor_tensor(x1_b2[:, q, :], x1[:, q, :], b2_wide[:, bass.ds(lang * D, D)], ALU.add
                                            ).then_inc(x1_b2_ready, 1)
                    if s.is_at_least(2):
                        pool.wait_ge(x2_ready, s.upto(2))
                    nc.gpsimd.tensor_tensor(x1_beta[:, q, :], x1[:, q, :], beta_wide[:, bass.ds(lang * D, D)], ALU.add
                                            ).then_inc(x1_beta_ready, 1)
                    if s.is_at_least(2):
                        pool.wait_ge(rows_mm, s.upto(2))
                    nc.gpsimd.tensor_tensor(rows_mix[:, q, :], rows_shift[:, :],
                                            zy_t[:, bass.ds(s.n, 1)].to_broadcast([P, P]), ALU.mult
                                            ).then_inc(rows_mix_ready, 1)

            run_slots(pool, slot, 0, B, 5, B - 2)


def kernel(x, itok_B_0_2, itok_B_0_8, condB_zX, condB_zY, condB_zR, itok_B_0_63, L0_cond_W1, L0_cond_b1, L0_cond_v,
           L1_cond_W1, L1_cond_b1, L1_cond_W2, L1_cond_b2, L1_cond_gamma, L1_cond_beta, L3_cond_W, L3_cond_b):
    import concourse.bacc as bacc
    from concourse.bass_utils import run_bass_kernel_spmd

    def tiles(w):
        w = np.asarray(w)
        *lead, rows, cols = w.shape
        w = np.moveaxis(w.reshape(*lead, rows // P, P, cols), -3, -2)
        return np.ascontiguousarray(w.reshape(*lead, P, rows // P * cols))

    x = np.ascontiguousarray(x)
    L, A, D = L1_cond_W2.shape
    arrays = {
        "x": x,
        "xT": tiles(x.transpose(0, 2, 1)),
        "kinds": np.asarray(itok_B_0_2)[:, None],
        "langs": np.asarray(itok_B_0_8)[:, None],
        "zx": np.asarray(condB_zX)[:, None],
        "zy": np.asarray(condB_zY)[:, None],
        "zr": np.asarray(condB_zR)[:, None],
        "cats": np.asarray(itok_B_0_63)[:, None],
        "w1a": tiles(L0_cond_W1),
        "b1a": np.asarray(L0_cond_b1)[:, None],
        "va": np.asarray(L0_cond_v)[:, None],
        "w1l": tiles(L1_cond_W1),
        "b1l": np.ascontiguousarray(np.asarray(L1_cond_b1).T),
        "w2l": np.ascontiguousarray(np.asarray(L1_cond_W2).transpose(1, 0, 2).reshape(A, L * D)),
        "b2l": np.asarray(L1_cond_b2),
        "gamma": np.asarray(L1_cond_gamma),
        "beta": np.asarray(L1_cond_beta),
        "w3": tiles(L3_cond_W),
        "b3": np.asarray(L3_cond_b),
    }
    arrays = {f"in_{k}": np.ascontiguousarray(v) for k, v in arrays.items()}
    nc = bacc.Bacc("TRN2", target_bir_lowering=False, num_devices=1, dynamic_dma_scratch_size=1024)
    args = [nc.dram_tensor(k, v.shape, mybir.dt.from_np(v.dtype), kind="ExternalInput").ap()
            for k, v in arrays.items()]
    out = nc.dram_tensor("out_x", x.shape, F32, kind="ExternalOutput").ap()
    cond_residual_kernel(nc, *args, out)
    r = run_bass_kernel_spmd(nc, [arrays], core_ids=[0])
    return r.results[0]["out_x"]
```

```python
import numpy as np
import concourse.bass as bass
from concourse import mybir
from contextlib import ExitStack

F32 = mybir.dt.float32
F32R = mybir.dt.float32r
BF16 = mybir.dt.bfloat16
I32 = mybir.dt.int32
ALU = mybir.AluOpType
ACT = mybir.ActivationFunctionType
AX = mybir.AxisListType

P = 128
NEG = -1e30
EPS = 1e-5
UNROLL = 4
ITEM, CAT, LANG, KIND, FRESH, WSLOT, NPARAM = 0, 1, 2, 3, 4, 5, 8
ROWS = {
    "sp": [(ITEM, 3), (ITEM, 1), (LANG, 1), (CAT, 0), (FRESH, 0), (WSLOT, 0), (CAT, -1), (ITEM, -3)],
    "pe": [(KIND, 1), (LANG, 0), (WSLOT, -2)],
    "act": [(FRESH, -1), (WSLOT, -1), (LANG, 0)],
    "dve": [(FRESH, -1), (WSLOT, -1), (LANG, -1)],
    "pool": [(LANG, 0)],
}
LEAD = 3


class Step:

    def __init__(self, first, turn):
        self.first, self.turn = first, turn

    def __add__(self, k):
        return Step(self.first + k, self.turn)

    def __sub__(self, k):
        return self + (-k)

    def times(self, k):
        return 0 if self.turn is None else self.turn * k

    @property
    def n(self):
        return self.first + self.times(UNROLL)

    def upto(self, back=0):
        return self.first + 1 - back + self.times(UNROLL)

    def dma(self, size=2):
        return 16 * (self.first // size + 1) + self.times(16 * UNROLL // size)

    def inside(self, count):
        return self.turn is not None or 0 <= self.first < count

    def ring(self, size):
        return self.first % size

    def is_at_least(self, k):
        return self.first >= k


def run_slots(eng, body, first, last, steady_first, steady_last):
    turns = (steady_last - steady_first + 1) // UNROLL
    for s in range(first, steady_first):
        body(Step(s, None))
    with eng.Fori(0, turns) as turn:
        for j in range(UNROLL):
            body(Step(steady_first + j, turn))
    for s in range(steady_first + turns * UNROLL, last + 1):
        body(Step(s, None))


def cond_residual_kernel(nc, x, xT, kinds, langs, zx, zy, zr, cats, w1a, b1a, va,
                         w1l, b1l, w2l, b2l, gamma, beta, w3, b3, out):
    B, S, D = x.shape
    A = w1a.shape[1] // (D // P)
    K = D // P
    L = gamma.shape[0]
    C = w3.shape[0]
    ctx = ExitStack()

    def sb(name, shape, dt=F32):
        return ctx.enter_context(nc.sbuf_tensor(name, shape, dt))

    def pb(name):
        return ctx.enter_context(nc.psum_tensor(name, [P, 512], F32))

    def sem(name):
        return ctx.enter_context(nc.semaphore(name))

    def ring_sems(name, size=2):
        return [sem(f"{name}{i}") for i in range(size)]

    with ctx:
        b3_parts_dram = nc.dram_tensor("b3_parts_dram", [C, 3, D], BF16, kind="Internal").ap()

        w1_attn = sb("w1_attn", [P, K * A])
        b1_attn = sb("b1_attn", [P, 1])
        v_col = sb("v_col", [P, 1])
        v_wide = sb("v_wide", [P, P])
        w2_all = sb("w2_all", [P, L * D])
        b1_all = sb("b1_all", [P, L])
        b2_wide = sb("b2_wide", [P, L * D])
        gamma_wide = sb("gamma_wide", [P, L * D])
        beta_wide = sb("beta_wide", [P, L * D])
        ident = sb("ident", [P, P])
        ident16 = sb("ident16", [P, P], BF16)
        masks16 = sb("masks16", [P, 3 * P], BF16)
        rows_shift = sb("rows_shift", [P, P])
        rows_shift_r = sb("rows_shift_r", [P, P], F32R)
        mark = {e: sb(f"{e}_mark", [P, 2 * K]) for e in ("act", "dve", "pool")}
        ones3 = sb("ones3", [3, P], BF16)
        iota_row = sb("iota_row", [P, P])
        iota_col = sb("iota_col", [P, 1])
        minus_half = sb("minus_half", [P, 1])
        ones2 = sb("ones2", [P, 2])
        count_t = sb("count_t", [P, B])
        zx_t = sb("zx_t", [P, B])
        zy_t = sb("zy_t", [P, B])
        nzr_t = sb("nzr_t", [P, B])
        c0_t = sb("c0_t", [P, B])
        kind_t = sb("kind_t", [P, B])
        params_by_item = sb("params_by_item", [P, NPARAM], I32)
        W = 8
        all_params = sb("all_params", [len(ROWS), (B + 2 * LEAD) * W], I32)
        slot_params = {e: all_params[i:i + 1, :] for i, e in enumerate(ROWS)}
        ids_col = sb("ids_col", [P, 3], I32)
        cat_row_i = sb("cat_row_i", [P, B], I32)
        vals = sb("vals", [P, 12])
        rank_col = sb("rank_col", [P, 1])
        key_col = sb("key_col", [P, 1])
        seen_col = sb("seen_col", [P, 1])
        fresh_col = sb("fresh_col", [P, 1])
        slot_i = sb("slot_i", [P, 2], I32)

        xs = sb("xs", [P, 2, D])
        xts = sb("xts", [P, 2, K, S])
        w1s = sb("w1s", [P, 2, K, A])
        w3s = sb("w3s", [P, 2 * K * D])
        w3_hi = sb("w3_hi", [P, 2 * K * D], F32R)
        w3_lo = sb("w3_lo", [P, 2 * K * D], F32R)
        b3s = sb("b3s", [3, 2, D], BF16)
        cat_row, key_row, less, same, place, tmp = (w3s[:, i * P:(i + 1) * P] for i in range(6))
        wide = w3s[:, 6 * P:10 * P]
        b3_f, b3_rest = w3s[0:C, 10 * P:10 * P + D], w3s[0:C, 10 * P + D:10 * P + 2 * D]
        b3_parts = w3s[0:C, 10 * P + 2 * D:10 * P + 4 * D].bitcast(BF16)
        attn = sb("attn", [P, 2, S])
        neg_max = sb("neg_max", [P, 2])
        probs = sb("probs", [P, 2, S])
        prob_sum = sb("prob_sum", [P, 2])
        denom = sb("denom", [P, 2])
        scale = sb("scale", [P, 2])
        probsT = sb("probsT", [P, 2, S])
        x1 = sb("x1", [P, 2, D])
        x1T = sb("x1T", [P, 2, D])
        x1_b2 = sb("x1_b2", [P, D])
        x1_beta = sb("x1_beta", [P, 2, D])
        hid = sb("hid", [P, 2, S])
        y = sb("y", [P, 2, D])
        y_sum = sb("y_sum", [P, 2])
        neg_mean = sb("neg_mean", [P, 2])
        square_junk = sb("square_junk", [P, D])
        var_sum = sb("var_sum", [P, 2])
        var_eps = sb("var_eps", [P, 2])
        rstd = sb("rstd", [P, 2])
        x2 = sb("x2", [P, 2, D + 2])
        react = sb("react", [P, D])
        neighbours = sb("neighbours", [P, D])
        x2_hi = sb("x2_hi", [P, 2, D], F32R)
        x2_lo = sb("x2_lo", [P, 2, D], F32R)
        x3 = sb("x3", [P, 4, D])
        x3T_hi = sb("x3T_hi", [P, 2, D], F32R)
        x3T_lo = sb("x3T_lo", [P, 2, D], F32R)
        res = sb("res", [P, 2, D])

        bank_small = pb("bank_small")
        ps_attn, ps_probsT = bank_small[:, 0:S], bank_small[:, S:2 * S]
        bank_middle = pb("bank_middle")
        ps_scores, ps_hid = bank_middle[:, 0:S], bank_middle[:, S:2 * S]
        ps_pool = pb("ps_pool")
        ps_x1T = pb("ps_x1T")
        ps_x3T = pb("ps_x3T")
        ps_adapt = pb("ps_adapt")
        ps_rows = pb("ps_rows")
        ps_out = pb("ps_out")

        tables_in = sem("tables_in")
        ids_in = sem("ids_in")
        b3_in = sem("b3_in")
        b3_parts_out = sem("b3_parts_out")
        params_in = sem("params_in")
        PARAMS_IN = 16 * sum(len(row) for row in ROWS.values())
        x_in, xT_in, w1_in = ring_sems("x_in"), ring_sems("xT_in"), ring_sems("w1_in")
        w3_in, b3row_in, res_out = ring_sems("w3_in"), ring_sems("b3row_in"), ring_sems("res_out")
        consts_made = sem("consts_made")
        prep = sem("prep")
        pool_prep = sem("pool_prep")
        params_zeroed = sem("params_zeroed")
        b3_split = sem("b3_split")
        fresh_made, slots_summed = sem("fresh_made"), sem("slots_summed")
        place_made, sorted_made, tables_made = sem("place_made"), sem("sorted_made"), sem("tables_made")
        params_made = sem("params_made")
        gconst = sem("gconst")
        attn_mm, scores_mm, probsT_mm, pool_mm = (sem(n) for n in ("attn_mm", "scores_mm", "probsT_mm", "pool_mm"))
        x1T_mm, hid_mm, adapt_mm, rows_mm, x3T_mm, out_mm = (
            sem(n) for n in ("x1T_mm", "hid_mm", "adapt_mm", "rows_mm", "x3T_mm", "out_mm"))
        attn_ready, probs_ready, probsT_ready, x1T_ready, var_ready, react_ready, x3T_hi_ready = (
            sem(n) for n in ("attn_ready", "probs_ready", "probsT_ready", "x1T_ready", "var_ready",
                             "react_ready", "x3T_hi_ready"))
        relu_ready, x2_hi_ready, w3_hi_ready = sem("relu_ready"), sem("x2_hi_ready"), sem("w3_hi_ready")
        x3T_lo_ready, x2_lo_ready, w3_lo_ready = sem("x3T_lo_ready"), sem("x2_lo_ready"), sem("w3_lo_ready")
        max_ready, denom_ready, scale_ready, x1_ready, y_ready, mean_ready, norm_ready = (
            sem(n) for n in ("max_ready", "denom_ready", "scale_ready", "x1_ready", "y_ready",
                             "mean_ready", "norm_ready"))
        x2_ready, partial_ready, x3_ready, res_ready = (
            sem(n) for n in ("x2_ready", "partial_ready", "x3_ready", "res_ready"))
        edges_ready, neighbours_ready, react_x2_ready, x1_b2_ready, x1_beta_ready = (
            sem(n) for n in ("edges_ready", "neighbours_ready", "react_x2_ready", "x1_b2_ready",
                             "x1_beta_ready"))
        vareps_ready, rstd_ready = sem("vareps_ready"), sem("rstd_ready")

        block = ctx.enter_context(nc.Block())

        tops = {ITEM: B - 1, CAT: C - 1, LANG: L - 1, KIND: 2, FRESH: 1, WSLOT: 1}

        def load_params(eng, name, s):
            row, why = ROWS[name], "the ids index the tables' rows, the rest is made here"
            _, values = nc.values_load_multi_w_load_instructions(
                slot_params[name][:, bass.ds((s + LEAD).n * W, len(row))], engines=[eng.engine],
                min_val=0, max_val=B - 1, skip_runtime_bounds_check_because=why)
            return [nc.s_assert_within(v, 0, tops[what], skip_runtime_bounds_check_because=why)
                    for v, (what, _) in zip(values, row)]

        @block.sync
        def _(sp):
            sp.dma_start(ids_col[:, 0:1], cats).then_inc(ids_in, 16)
            sp.dma_start(ids_col[:, 1:2], langs).then_inc(ids_in, 16)
            sp.dma_start(ids_col[:, 2:3], kinds).then_inc(ids_in, 16)
            sp.dma_start(vals[:, 4:5], zx).then_inc(ids_in, 16)
            sp.dma_start(vals[:, 5:6], zy).then_inc(ids_in, 16)
            sp.dma_start(vals[:, 6:7], zr).then_inc(ids_in, 16)
            sp.dma_start(cat_row_i[:, :], cats.rearrange("b o -> (o b)").partition_broadcast(P)).then_inc(ids_in, 16)
            sp.dma_start(v_col[:, :], va).then_inc(ids_in, 16)
            sp.dma_start(b3_f[:, :], b3).then_inc(b3_in, 16)
            sp.dma_start(w1_attn[:, :], w1a).then_inc(tables_in, 16)
            sp.dma_start(b1_attn[:, :], b1a).then_inc(tables_in, 16)
            sp.dma_start(b1_all[:, :], b1l).then_inc(tables_in, 16)
            sp.dma_start(w2_all[:, :], w2l).then_inc(tables_in, 16)
            for table, src in ((b2_wide, b2l), (gamma_wide, gamma), (beta_wide, beta)):
                sp.dma_start(table[:, :], src.rearrange("l d -> (l d)").partition_broadcast(P)).then_inc(tables_in, 16)
            sp.wait_ge(b3_split, 1)
            sp.dma_start(b3_parts_dram, b3_parts[:, 0:3 * D].rearrange("c (t d) -> c t d", t=3)).then_inc(b3_parts_out, 16)
            sp.wait_ge(params_made, 1)
            sp.wait_ge(params_zeroed, 1)
            with nc.allow_non_contiguous_dma(reason="a few hundred words, once"):
                for name, row in ROWS.items():
                    table = slot_params[name].rearrange("o (r w) -> o r w", w=W)
                    for k, (what, ahead) in enumerate(row):
                        sp.dma_start(table[:, LEAD - ahead:LEAD - ahead + B, k:k + 1],
                                     params_by_item[:, what:what + 1]).then_inc(params_in, 16)
            sp.wait_ge(params_in, PARAMS_IN)
            sp.wait_ge(b3_parts_out, 16)
            sp.wait_ge(tables_made, 1)

            def load_xT(a, item):
                r = a.ring(2)
                if a.is_at_least(2):
                    sp.wait_ge(attn_mm, a.upto(2))
                sp.dma_start(xts[:, r], xT[bass.ds(item, 1)].rearrange("o p (k s) -> p (o k) s", k=K)
                             ).then_inc(xT_in[r], 16)

            def load_x(a, item, lang):
                r = a.ring(2)
                if a.is_at_least(2):
                    sp.wait_ge(x1_ready, a.upto(2))
                sp.dma_start(xs[:, r], x[bass.ds(item, 1)].rearrange("o s d -> s (o d)")).then_inc(x_in[r], 16)
                if a.is_at_least(2):
                    sp.wait_ge(hid_mm, a.upto(2))
                sp.dma_start(w1s[:, r], w1l[bass.ds(lang, 1)].rearrange("o p (k a) -> p (o k) a", k=K)
                             ).then_inc(w1_in[r], 16)

            def load_w3(c, cat, fresh, wslot):
                r = c.ring(2)
                if c.is_at_least(2):
                    sp.wait_ge(w3_hi_ready, c.upto(2) * K)
                    sp.wait_ge(w3_lo_ready, c.upto(2) * K)
                sp.dma_start(w3s[:, bass.ds(wslot * (K * D), K * D)],
                             w3[bass.ds(cat, 1)].rearrange("o p n -> p (o n)"),
                             cond=fresh, bounds_check="skip_entire_dma").then_inc(w3_in[r], 16)

            def load_b3(c, cat):
                r = c.ring(2)
                if c.is_at_least(2):
                    sp.wait_ge(out_mm, c.upto(2))
                sp.dma_start(b3s[:, r], b3_parts_dram[bass.ds(cat, 1)].rearrange("o t d -> t (o d)")
                             ).then_inc(b3row_in[r], 16)

            def store(o, item):
                sp.wait_ge(res_ready, o.upto())
                sp.dma_start(out[bass.ds(item, 1)].rearrange("o s d -> s (o d)"), res[:, o.ring(2)]
                             ).then_inc(res_out[o.ring(2)], 16)

            def slot(s):
                item_p3, item_p1, lang_p1, cat, fresh, wslot, cat_m1, item_m3 = load_params(sp, "sp", s)
                if (s + 3).inside(B):
                    load_xT(s + 3, item_p3)
                if (s + 1).inside(B):
                    load_x(s + 1, item_p1, lang_p1)
                if s.inside(B):
                    load_w3(s, cat, fresh, wslot)
                if (s - 1).inside(B):
                    load_b3(s - 1, cat_m1)
                if (s - 3).inside(B):
                    store(s - 3, item_m3)

            run_slots(sp, slot, -3, B + 2, 5, B - 4)
            for r in range(2):
                sp.wait_ge(res_out[r], 16 * (B // 2))
                sp.wait_ge(w3_in[r], 16 * (B // 2))

        @block.tensor
        def _(pe):
            pe.wait_ge(fresh_made, 1)
            pe.matmul(ps_pool[:, 0:1], less[:, :], fresh_col[:, :], start=True, stop=True).then_inc(slots_summed, 1)
            pe.wait_ge(place_made, 1)
            pe.matmul(ps_adapt[:, 0:NPARAM], place[:, :], vals[:, 0:NPARAM], start=True, stop=True
                      ).then_inc(sorted_made, 1)
            for i in range(4):
                mm = pe.matmul(ps_rows[:, i * P:(i + 1) * P], wide[:, i * P:(i + 1) * P], place[:, :],
                               start=True, stop=True)
            mm.then_inc(sorted_made, 1)
            pe.wait_ge(tables_made, 1)
            pe.wait_ge(gconst, 1)
            pe.wait_ge(tables_in, 16 * 7)
            pe.wait_ge(params_in, PARAMS_IN)

            def attn_project(a):
                r = a.ring(2)
                pe.wait_ge(xT_in[r], a.dma())
                if a.is_at_least(1):
                    pe.wait_ge(attn_ready, a.upto(1))
                if a.is_at_least(2):
                    pe.wait_ge(probsT_ready, a.upto(2))
                for k in range(K):
                    mm = pe.matmul(ps_attn, w1_attn[:, k * A:(k + 1) * A], xts[:, r, k, :],
                                   start=(k == 0), stop=(k == K - 1))
                mm.then_inc(attn_mm, 1)

            def attn_scores(b, kind):
                pe.wait_ge(attn_ready, b.upto())
                if b.is_at_least(1):
                    pe.wait_ge(probs_ready, b.upto(1))
                if b.is_at_least(2):
                    pe.wait_ge(relu_ready, b.upto(2))
                pe.matmul(ps_scores, v_wide[:, :], attn[:, b.ring(2), :], start=True, stop=False)
                pe.matmul(ps_scores, ident16[:, :], masks16[:, bass.ds(kind * P, P)], start=False, stop=True
                          ).then_inc(scores_mm, 1)

            def probs_transpose(c):
                pe.wait_ge(probs_ready, c.upto())
                if (c + 1).inside(B):
                    pe.wait_ge(attn_ready, (c + 1).upto())
                pe.transpose(ps_probsT, probs[:, c.ring(2), :], ident[:, :]).then_inc(probsT_mm, 1)

            def pool(d):
                pe.wait_ge(probsT_ready, d.upto())
                pe.wait_ge(x_in[d.ring(2)], d.dma())
                if d.is_at_least(1):
                    pe.wait_ge(x1_ready, d.upto(1))
                pe.matmul(ps_pool[:, :], probsT[:, d.ring(2), :], xs[:, d.ring(2), :], start=True, stop=True
                          ).then_inc(pool_mm, 1)

            def x1_transpose(e):
                pe.wait_ge(x1_ready, e.upto())
                if e.is_at_least(1):
                    pe.wait_ge(x1T_ready, e.upto(1))
                for k in range(K):
                    mm = pe.transpose(ps_x1T[:, k * P:(k + 1) * P], x1[:, e.ring(2), k * P:(k + 1) * P], ident[:, :])
                mm.then_inc(x1T_mm, 1)

            def x3_transpose(i):
                pe.wait_ge(x3_ready, i.upto())
                if i.is_at_least(1):
                    pe.wait_ge(x3T_lo_ready, i.upto(1))
                for k in range(K):
                    mm = pe.transpose(ps_x3T[:, k * P:(k + 1) * P], x3[:, i.ring(4), k * P:(k + 1) * P], ident[:, :])
                mm.then_inc(x3T_mm, 1)

            def adapter_down(f):
                pe.wait_ge(x1T_ready, f.upto())
                pe.wait_ge(w1_in[f.ring(2)], f.dma())
                if f.is_at_least(1):
                    pe.wait_ge(relu_ready, f.upto(1))
                if (f + 1).inside(B):
                    pe.wait_ge(probs_ready, (f + 1).upto())
                for k in range(K):
                    mm = pe.matmul(ps_hid, w1s[:, f.ring(2), k, :], x1T[:, f.ring(2), k * P:(k + 1) * P],
                                   start=(k == 0), stop=(k == K - 1))
                mm.then_inc(hid_mm, 1)

            def adapter_up(g, lang):
                pe.wait_ge(relu_ready, g.upto())
                if g.is_at_least(1):
                    pe.wait_ge(y_ready, g.upto(1))
                pe.matmul(ps_adapt[:, :], hid[:, g.ring(2), :], w2_all[:, bass.ds(lang * D, D)],
                          start=True, stop=True).then_inc(adapt_mm, 1)

            def rows_laplacian(h):
                pe.wait_ge(x2_hi_ready, h.upto())
                pe.wait_ge(x2_lo_ready, h.upto())
                if h.is_at_least(1):
                    pe.wait_ge(partial_ready, h.upto(1))
                pe.matmul(ps_rows[:, :], rows_shift_r[:, :], x2_hi[:, h.ring(2), :], start=True, stop=False)
                pe.matmul(ps_rows[:, :], rows_shift_r[:, :], x2_lo[:, h.ring(2), :], start=False, stop=True
                          ).then_inc(rows_mm, 1)

            def category_high(j, wslot):
                pe.wait_ge(x3T_hi_ready, j.upto())
                pe.wait_ge(w3_hi_ready, j.upto() * K)
                pe.wait_ge(w3_lo_ready, j.upto() * K)
                if j.is_at_least(1):
                    pe.wait_ge(res_ready, j.upto(1))
                for k in range(K):
                    for part in (w3_hi, w3_lo):
                        pe.matmul(ps_out[:, :], x3T_hi[:, j.ring(2), k * P:(k + 1) * P],
                                  part[:, bass.ds(wslot * (K * D) + k * D, D)],
                                  start=(k == 0 and part is w3_hi), stop=False)

            def category_low(j, wslot):
                pe.wait_ge(x3T_lo_ready, j.upto())
                for k in range(K):
                    pe.matmul(ps_out[:, :], x3T_lo[:, j.ring(2), k * P:(k + 1) * P],
                              w3_hi[:, bass.ds(wslot * (K * D) + k * D, D)], start=False, stop=False)
                pe.wait_ge(b3row_in[j.ring(2)], j.dma())
                pe.matmul(ps_out[:, :], ones3[:, :], b3s[:, j.ring(2), :], start=False, stop=True
                          ).then_inc(out_mm, 1)

            def slot(s):
                j = s - 2
                kind, lang, wslot = load_params(pe, "pe", s)
                if s.inside(B):
                    pool(s)
                if (s + 2).inside(B):
                    attn_project(s + 2)
                if j.inside(B):
                    x3_transpose(j)
                if s.inside(B):
                    x1_transpose(s)
                if (s + 1).inside(B):
                    attn_scores(s + 1, kind)
                if j.inside(B):
                    category_high(j, wslot)
                if (s + 1).inside(B):
                    probs_transpose(s + 1)
                if s.inside(B):
                    adapter_down(s)
                if j.inside(B):
                    category_low(j, wslot)
                if (s - 1).inside(B):
                    rows_laplacian(s - 1)
                if s.inside(B):
                    adapter_up(s, lang)

            run_slots(pe, slot, -2, B + 1, 6, B - 3)

        @block.scalar
        def _(act):
            act.wait_ge(tables_made, 1)
            act.wait_ge(tables_in, 16 * 7)

            def high_x3T(i):
                act.wait_ge(x3T_mm, i.upto())
                if i.is_at_least(2):
                    act.wait_ge(out_mm, i.upto(2))
                nc.scalar.activation(x3T_hi[:, i.ring(2), :], ps_x3T[:, :], ACT.Copy).then_inc(x3T_hi_ready, 1)

            def variance(h):
                q = h.ring(2)
                act.wait_ge(mean_ready, h.upto())
                if h.is_at_least(2):
                    act.wait_ge(vareps_ready, h.upto(2))
                nc.scalar.activation(square_junk[:, :], y[:, q, :], ACT.Square, bias=neg_mean[:, q:q + 1],
                                     accum_out=var_sum[:, q:q + 1]).then_inc(var_ready, 1)

            def high_x2(h):
                act.wait_ge(x2_ready, h.upto())
                if h.is_at_least(2):
                    act.wait_ge(rows_mm, h.upto(2))
                nc.scalar.activation(x2_hi[:, h.ring(2), :], x2[:, h.ring(2), 1:D + 1], ACT.Copy
                                     ).then_inc(x2_hi_ready, 1)

            def reaction(h):
                if h.is_at_least(1):
                    act.wait_ge(x3_ready, h.upto(1))
                nc.scalar.activation(react[:, :], x2[:, h.ring(2), 1:D + 1], ACT.Identity,
                                     bias=c0_t[:, bass.ds(h.n, 1)], scale=nzr_t[:, bass.ds(h.n, 1)]
                                     ).then_inc(react_ready, 1)

            def move_x1T(s):
                act.wait_ge(x1T_mm, s.upto())
                if s.is_at_least(2):
                    act.wait_ge(hid_mm, s.upto(2))
                nc.scalar.activation(x1T[:, s.ring(2), :], ps_x1T[:, :], ACT.Copy).then_inc(x1T_ready, 1)

            def attn_tanh(a):
                act.wait_ge(attn_mm, a.upto())
                if a.is_at_least(2):
                    act.wait_ge(scores_mm, a.upto(2))
                nc.scalar.activation(attn[:, a.ring(2), :], ps_attn, ACT.Tanh, bias=b1_attn[:, 0:1]
                                     ).then_inc(attn_ready, 1)

            def exponentials(b):
                act.wait_ge(max_ready, b.upto())
                if b.is_at_least(2):
                    act.wait_ge(probsT_mm, b.upto(2))
                    act.wait_ge(denom_ready, b.upto(2))
                nc.scalar.activation(probs[:, b.ring(2), :], ps_scores, ACT.Exp,
                                     bias=neg_max[:, b.ring(2):b.ring(2) + 1],
                                     accum_out=prob_sum[:, b.ring(2):b.ring(2) + 1]).then_inc(probs_ready, 1)

            def move_probsT(b):
                act.wait_ge(probsT_mm, b.upto())
                if b.is_at_least(2):
                    act.wait_ge(pool_mm, b.upto(2))
                nc.scalar.activation(probsT[:, b.ring(2), :], ps_probsT, ACT.Copy).then_inc(probsT_ready, 1)

            def relu(f, lang):
                act.wait_ge(hid_mm, f.upto())
                if f.is_at_least(2):
                    act.wait_ge(adapt_mm, f.upto(2))
                nc.scalar.activation(hid[:, f.ring(2), :], ps_hid, ACT.Relu, bias=b1_all[:, bass.ds(lang, 1)]
                                     ).then_inc(relu_ready, 1)

            def high_w3(c, fresh, wslot, k):
                with act.If(fresh):
                    if k == 0:
                        act.wait_ge(w3_in[c.ring(2)], c.dma())
                        if c.is_at_least(2):
                            act.wait_ge(out_mm, c.upto(2))
                    piece = bass.ds(wslot * (K * D) + k * D, D)
                    nc.scalar.activation(w3_hi[:, piece], w3s[:, piece], ACT.Copy).then_inc(w3_hi_ready, 1)
                with act.Else():
                    column = slice(c.ring(2) * K + k, c.ring(2) * K + k + 1)
                    nc.scalar.activation(mark["act"][:, column], b1_attn[:, :], ACT.Copy).then_inc(w3_hi_ready, 1)

            def slot(s):
                c = s - 1
                fresh, wslot, lang = load_params(act, "act", s)
                if c.inside(B):
                    high_w3(c, fresh, wslot, 0)
                    high_w3(c, fresh, wslot, 1)
                    variance(s - 1)
                if (s + 2).inside(B):
                    attn_tanh(s + 2)
                if (s - 2).inside(B):
                    high_x3T(s - 2)
                if s.inside(B):
                    move_x1T(s)
                if c.inside(B):
                    high_w3(c, fresh, wslot, 2)
                if (s + 1).inside(B):
                    exponentials(s + 1)
                if c.inside(B):
                    high_x2(s - 1)
                    reaction(s - 1)
                if (s + 1).inside(B):
                    move_probsT(s + 1)
                if s.inside(B):
                    relu(s, lang)
                if c.inside(B):
                    high_w3(c, fresh, wslot, 3)

            run_slots(act, slot, -2, B + 1, 6, B - 3)

        @block.vector
        def _(dve):
            steps = [0]

            def then(ins):
                steps[0] += 1
                ins.then_inc(prep, 1)
                dve.wait_ge(prep, steps[0])

            dve.wait_ge(ids_in, 16 * 8)
            dve.wait_ge(consts_made, 1)
            nc.vector.memset(ones3[:, :], 1.0)
            nc.vector.memset(minus_half[:, :], -0.5)
            nc.vector.memset(ones2[:, :], 1.0)
            nc.vector.tensor_copy(vals[:, 0:1], iota_col[:, :])
            nc.vector.tensor_copy(vals[:, 1:4], ids_col[:, :])
            nc.vector.tensor_copy(ident16[:, :], ident[:, :])
            then(nc.vector.tensor_copy(cat_row[:, :], cat_row_i[:, :]))
            nc.vector.scalar_tensor_tensor(key_row[:, :], cat_row[:, :], float(B), iota_row[:, :], ALU.mult, ALU.add)
            then(nc.vector.scalar_tensor_tensor(key_col[:, :], vals[:, 1:2], float(B), iota_col[:, :], ALU.mult, ALU.add))
            then(nc.vector.tensor_scalar(less[:, :], key_row[:, :], key_col[:, 0:1], None, ALU.is_lt))
            nc.vector.tensor_reduce(rank_col[:, :], less[:, :], AX.X, ALU.add)
            then(nc.vector.tensor_scalar(same[:, :], cat_row[:, :], vals[:, 1:2], None, ALU.is_equal))
            then(nc.vector.tensor_tensor(same[:, :], same[:, :], less[:, :], ALU.mult))
            then(nc.vector.tensor_reduce(seen_col[:, :], same[:, :], AX.X, ALU.add))
            nc.vector.tensor_scalar(fresh_col[:, :], seen_col[:, :], 0.0, None, ALU.is_equal)
            then(nc.vector.tensor_scalar(less[:, :], cat_row[:, :], vals[:, 1:2], None, ALU.is_gt))
            nc.vector.tensor_copy(vals[:, 7:8], vals[:, 4:5])
            nc.vector.tensor_copy(vals[:, 8:9], vals[:, 5:6])
            then(nc.vector.tensor_copy(vals[:, 9:10], vals[:, 6:7]))
            nc.vector.tensor_scalar(wide[:, 0:P], ident[:, :], 0.0, vals[:, 7:8], ALU.mult, ALU.add)
            nc.vector.tensor_scalar(wide[:, P:2 * P], ident[:, :], 0.0, vals[:, 8:9], ALU.mult, ALU.add)
            nc.vector.tensor_scalar(wide[:, 2 * P:3 * P], ident[:, :], 0.0, vals[:, 9:10], ALU.mult, ALU.add)
            nc.vector.tensor_scalar(wide[:, 3 * P:4 * P], ident[:, :], 0.0, vals[:, 3:4], ALU.mult, ALU.add)
            nc.vector.tensor_scalar(v_wide[:, :], ident[:, :], 0.0, v_col[:, 0:1], ALU.mult, ALU.add)
            nc.vector.tensor_copy(vals[:, FRESH:FRESH + 1], fresh_col[:, :]).then_inc(fresh_made, 1)
            dve.wait_ge(slots_summed, 1)
            then(nc.vector.tensor_copy(slot_i[:, 0:1], ps_pool[:, 0:1]))
            then(nc.vector.tensor_scalar(slot_i[:, 1:2], slot_i[:, 0:1], 1, None, ALU.bitwise_and))
            nc.vector.tensor_copy(vals[:, WSLOT:WSLOT + 1], slot_i[:, 1:2])
            nc.vector.memset(vals[:, 6:8], 0.0)
            nc.vector.tensor_scalar(place[:, :], iota_row[:, :], rank_col[:, 0:1], None, ALU.is_equal
                                    ).then_inc(place_made, 1)
            dve.wait_ge(sorted_made, 1)
            nc.vector.tensor_copy(params_by_item[:, :], ps_adapt[:, 0:NPARAM]).then_inc(params_made, 1)
            dve.wait_ge(sorted_made, 2)
            nc.vector.tensor_copy(zx_t[:, :], ps_rows[:, 0:P])
            nc.vector.tensor_copy(zy_t[:, :], ps_rows[:, P:2 * P])
            nc.vector.tensor_scalar(nzr_t[:, :], ps_rows[:, 2 * P:3 * P], -1.0, None, ALU.mult)
            then(nc.vector.tensor_copy(kind_t[:, :], ps_rows[:, 3 * P:4 * P]))
            then(nc.vector.tensor_tensor(tmp[:, :], zx_t[:, :], zy_t[:, :], ALU.add))
            then(nc.vector.tensor_scalar(tmp[:, :], tmp[:, :], -2.0, 1.0, ALU.mult, ALU.add))
            then(nc.vector.tensor_tensor(c0_t[:, :], tmp[:, :], nzr_t[:, :], ALU.subtract))
            nc.vector.tensor_scalar(key_col[:, :], iota_col[:, :], 1.0, None, ALU.add)
            nc.vector.tensor_scalar(seen_col[:, :], iota_col[:, :], -1.0, float(S), ALU.mult, ALU.add)
            then(nc.vector.tensor_scalar(tmp[:, :], kind_t[:, :], 0.0, None, ALU.is_equal))
            then(nc.vector.tensor_scalar(count_t[:, :], tmp[:, :], key_col[:, 0:1], None, ALU.mult))
            then(nc.vector.tensor_scalar(tmp[:, :], kind_t[:, :], 1.0, None, ALU.is_equal))
            then(nc.vector.scalar_tensor_tensor(count_t[:, :], tmp[:, :], seen_col[:, 0:1], count_t[:, :],
                                                ALU.mult, ALU.add))
            then(nc.vector.tensor_scalar(tmp[:, :], kind_t[:, :], 1.5, float(S - 1), ALU.is_gt, ALU.mult))
            then(nc.vector.tensor_tensor(count_t[:, :], count_t[:, :], tmp[:, :], ALU.add))
            dve.wait_ge(b3_in, 16)
            then(nc.vector.tensor_copy(b3_parts[:, 0:D], b3_f[:, :]))
            then(nc.vector.tensor_tensor(b3_rest[:, :], b3_f[:, :], b3_parts[:, 0:D], ALU.subtract))
            then(nc.vector.tensor_copy(b3_parts[:, D:2 * D], b3_rest[:, :]))
            then(nc.vector.tensor_tensor(b3_rest[:, :], b3_rest[:, :], b3_parts[:, D:2 * D], ALU.subtract))
            nc.vector.tensor_copy(b3_parts[:, 2 * D:3 * D], b3_rest[:, :]).then_inc(b3_split, 1)
            dve.wait_ge(gconst, 1)
            nc.vector.tensor_copy(rows_shift_r[:, :], rows_shift[:, :])
            dve.wait_ge(b3_split, 1)
            nc.vector.memset(mark["dve"][:, :], 0.0).then_inc(tables_made, 1)
            dve.wait_ge(tables_in, 16 * 7)
            dve.wait_ge(params_in, PARAMS_IN)

            def add_adapted(h):
                q = h.ring(2)
                dve.wait_ge(adapt_mm, h.upto())
                dve.wait_ge(x1_b2_ready, h.upto())
                nc.vector.scalar_tensor_tensor(y[:, q, :], ps_adapt[:, :], 1.0, x1_b2[:, :], ALU.mult, ALU.add,
                                               accum_out=y_sum[:, q:q + 1]).then_inc(y_ready, 1)
                dve.wait_ge(y_ready, h.upto())
                nc.vector.tensor_scalar(neg_mean[:, q:q + 1], y_sum[:, q:q + 1], -1.0 / D, None, ALU.mult
                                        ).then_inc(mean_ready, 1)

            def add_pooled(s):
                q = s.ring(2)
                dve.wait_ge(pool_mm, s.upto())
                dve.wait_ge(scale_ready, s.upto())
                if s.is_at_least(2):
                    dve.wait_ge(x1T_mm, s.upto(2))
                    dve.wait_ge(x1_beta_ready, s.upto(2))
                    dve.wait_ge(x1_b2_ready, s.upto(2))
                nc.vector.scalar_tensor_tensor(x1[:, q, :], ps_pool[:, :], scale[:, q:q + 1], xs[:, s.ring(2), :],
                                               ALU.mult, ALU.add).then_inc(x1_ready, 1)

            def result(o):
                dve.wait_ge(out_mm, o.upto())
                if o.is_at_least(2):
                    dve.wait_ge(res_out[o.ring(2)], (o - 2).dma())
                nc.vector.tensor_tensor(res[:, o.ring(2), :], ps_out[:, :], x3[:, o.ring(4), :], ALU.add
                                        ).then_inc(res_ready, 1)

            def low_x3T(i):
                dve.wait_ge(x3T_hi_ready, i.upto())
                if i.is_at_least(2):
                    dve.wait_ge(out_mm, i.upto(2))
                nc.vector.tensor_tensor(x3T_lo[:, i.ring(2), :], ps_x3T[:, :], x3T_hi[:, i.ring(2), :].bitcast(F32),
                                        ALU.subtract).then_inc(x3T_lo_ready, 1)

            def center(h, lang):
                q = h.ring(2)
                dve.wait_ge(var_ready, h.upto())
                if h.is_at_least(2):
                    dve.wait_ge(rstd_ready, h.upto(2))
                nc.vector.tensor_scalar(var_eps[:, q:q + 1], var_sum[:, q:q + 1], 1.0 / D, EPS,
                                        ALU.mult, ALU.add).then_inc(vareps_ready, 1)
                nc.vector.scalar_tensor_tensor(y[:, q, :], y[:, q, :], neg_mean[:, q:q + 1],
                                               gamma_wide[:, bass.ds(lang * D, D)], ALU.add, ALU.mult
                                               ).then_inc(norm_ready, 1)

            def normalize(h):
                q = h.ring(2)
                dve.wait_ge(norm_ready, h.upto())
                dve.wait_ge(rstd_ready, h.upto())
                dve.wait_ge(x1_beta_ready, h.upto())
                if h.is_at_least(2):
                    dve.wait_ge(react_ready, h.upto(2))
                    dve.wait_ge(react_x2_ready, h.upto(2))
                    dve.wait_ge(neighbours_ready, h.upto(2))
                nc.vector.scalar_tensor_tensor(x2[:, q, 1:D + 1], y[:, q, :], rstd[:, q:q + 1], x1_beta[:, q, :],
                                               ALU.mult, ALU.add).then_inc(x2_ready, 1)

            def low_x2(h):
                q = h.ring(2)
                dve.wait_ge(x2_hi_ready, h.upto())
                if h.is_at_least(2):
                    dve.wait_ge(rows_mm, h.upto(2))
                nc.vector.tensor_tensor(x2_lo[:, q, :], x2[:, q, 1:D + 1], x2_hi[:, q, :].bitcast(F32), ALU.subtract
                                        ).then_inc(x2_lo_ready, 1)

            def low_w3(c, fresh, wslot, k):
                with dve.If(fresh):
                    dve.wait_ge(w3_hi_ready, c.upto() * K - (K - 1 - k))
                    if k == 0 and c.is_at_least(2):
                        dve.wait_ge(out_mm, c.upto(2))
                    piece = bass.ds(wslot * (K * D) + k * D, D)
                    nc.vector.tensor_tensor(w3_lo[:, piece], w3s[:, piece], w3_hi[:, piece].bitcast(F32),
                                            ALU.subtract).then_inc(w3_lo_ready, 1)
                with dve.Else():
                    column = slice(c.ring(2) * K + k, c.ring(2) * K + k + 1)
                    nc.vector.memset(mark["dve"][:, column], 0.0).then_inc(w3_lo_ready, 1)

            def row_max(b):
                p = b.ring(2)
                dve.wait_ge(scores_mm, b.upto())
                if b.is_at_least(2):
                    dve.wait_ge(probs_ready, b.upto(2))
                nc.vector.tensor_reduce(neg_max[:, p:p + 1], ps_scores, AX.X, ALU.max, negate=True
                                        ).then_inc(max_ready, 1)

            def row_scale(b):
                p = b.ring(2)
                dve.wait_ge(probs_ready, b.upto())
                nc.vector.tensor_tensor(denom[:, p:p + 1], prob_sum[:, p:p + 1], count_t[:, bass.ds(b.n, 1)],
                                        ALU.mult).then_inc(denom_ready, 1)
                dve.wait_ge(denom_ready, b.upto())
                nc.vector.reciprocal(scale[:, p:p + 1], denom[:, p:p + 1]).then_inc(scale_ready, 1)

            def add_rows(h):
                dve.wait_ge(rows_mm, h.upto())
                dve.wait_ge(react_x2_ready, h.upto())
                nc.vector.scalar_tensor_tensor(react[:, :], ps_rows[:, :], zy_t[:, bass.ds(h.n, 1)], react[:, :],
                                               ALU.mult, ALU.add).then_inc(partial_ready, 1)

            def add_columns(h):
                dve.wait_ge(partial_ready, h.upto())
                dve.wait_ge(neighbours_ready, h.upto())
                if h.is_at_least(4):
                    dve.wait_ge(x3T_mm, h.upto(4))
                nc.vector.scalar_tensor_tensor(x3[:, h.ring(4), :], neighbours[:, :], zx_t[:, bass.ds(h.n, 1)],
                                               react[:, :], ALU.mult, ALU.add).then_inc(x3_ready, 1)

            def slot(s):
                c = s - 1
                fresh, wslot, lang = load_params(dve, "dve", s)
                if c.inside(B):
                    add_adapted(s - 1)
                if s.inside(B):
                    add_pooled(s)
                if (s - 3).inside(B):
                    result(s - 3)
                if c.inside(B):
                    center(s - 1, lang)
                if (s + 1).inside(B):
                    row_max(s + 1)
                if c.inside(B):
                    normalize(s - 1)
                if (s - 2).inside(B):
                    low_x3T(s - 2)
                if c.inside(B):
                    low_w3(c, fresh, wslot, 0)
                    low_x2(s - 1)
                    low_w3(c, fresh, wslot, 1)
                if (s + 1).inside(B):
                    row_scale(s + 1)
                if c.inside(B):
                    low_w3(c, fresh, wslot, 2)
                    add_rows(s - 1)
                    low_w3(c, fresh, wslot, 3)
                    add_columns(s - 1)

            run_slots(dve, slot, -1, B + 2, 7, B - 2)

        @block.gpsimd
        def _(pool):
            steps = [0]

            def then(ins):
                steps[0] += 1
                ins.then_inc(pool_prep, 1)
                pool.wait_ge(pool_prep, steps[0])

            nc.gpsimd.memset(all_params[:, :], 0).then_inc(params_zeroed, 1)
            nc.gpsimd.memset(ident[:, :], 0.0)
            nc.gpsimd.memset(rows_shift[:, :], 0.0)
            nc.gpsimd.memset(masks16[:, :], 0.0)
            nc.gpsimd.iota(iota_row[:, :], [[1, P]], base=0, channel_multiplier=0,
                           allow_small_or_imprecise_dtypes=True)
            then(nc.gpsimd.iota(iota_col[:, :], [[0, 1]], base=0, channel_multiplier=1,
                                allow_small_or_imprecise_dtypes=True))

            nc.gpsimd.affine_select(ident[:, :], ident[:, :], [[-1, P]], ALU.not_equal, 1.0, base=0,
                                    channel_multiplier=1).then_inc(consts_made, 1)
            for base in (1, -1):
                then(nc.gpsimd.affine_select(rows_shift[:, :], rows_shift[:, :], [[-1, P]], ALU.not_equal, 1.0,
                                             base=base, channel_multiplier=1))
            for to, source in ((0, 1), (P - 1, P - 2)):
                then(nc.gpsimd.affine_select(rows_shift[:, to:to + 1], rows_shift[:, to:to + 1], [[0, 1]],
                                             ALU.not_equal, 2.0, base=-source, channel_multiplier=1))
            for m, (step, mult, op) in enumerate(((-1, 1, ALU.is_ge), (1, -1, ALU.is_ge), (-1, 1, ALU.not_equal))):
                then(nc.gpsimd.affine_select(masks16[:, m * P:(m + 1) * P], masks16[:, m * P:(m + 1) * P], [[step, P]],
                                             op, NEG, base=0, channel_multiplier=mult))
            nc.gpsimd.memset(mark["pool"][:, :], 0.0).then_inc(gconst, 1)
            pool.wait_ge(tables_made, 1)
            pool.wait_ge(tables_in, 16 * 7)
            pool.wait_ge(params_in, PARAMS_IN)

            def inverse_std(h):
                q = h.ring(2)
                pool.wait_ge(vareps_ready, h.upto())
                if h.is_at_least(2):
                    pool.wait_ge(x2_ready, h.upto(2))
                nc.gpsimd.tensor_tensor(rstd[:, q:q + 1], var_eps[:, q:q + 1], minus_half[:, :], ALU.pow
                                        ).then_inc(rstd_ready, 1)

            def columns_and_reaction(h):
                q = h.ring(2)
                pool.wait_ge(x2_ready, h.upto())
                ends = x2[:, q, 2:D:D - 3]
                nc.gpsimd.tensor_tensor(x2[:, q, 0:D + 2:D + 1], ends, ones2[:, :], ALU.mult).then_inc(edges_ready, 1)
                pool.wait_ge(edges_ready, h.upto())
                if h.is_at_least(1):
                    pool.wait_ge(x3_ready, h.upto(1))
                nc.gpsimd.tensor_tensor(neighbours[:, :], x2[:, q, 0:D], x2[:, q, 2:D + 2], ALU.add
                                        ).then_inc(neighbours_ready, 1)
                pool.wait_ge(react_ready, h.upto())
                nc.gpsimd.tensor_tensor(react[:, :], react[:, :], x2[:, q, 1:D + 1], ALU.mult
                                        ).then_inc(react_x2_ready, 1)

            def add_b2(s, lang):
                pool.wait_ge(x1_ready, s.upto())
                if s.is_at_least(1):
                    pool.wait_ge(y_ready, s.upto(1))
                nc.gpsimd.tensor_tensor(x1_b2[:, :], x1[:, s.ring(2), :], b2_wide[:, bass.ds(lang * D, D)], ALU.add
                                        ).then_inc(x1_b2_ready, 1)

            def add_beta(s, lang):
                if s.is_at_least(2):
                    pool.wait_ge(x2_ready, s.upto(2))
                nc.gpsimd.tensor_tensor(x1_beta[:, s.ring(2), :], x1[:, s.ring(2), :],
                                        beta_wide[:, bass.ds(lang * D, D)], ALU.add).then_inc(x1_beta_ready, 1)

            def slot(s):
                lang, = load_params(pool, "pool", s)
                if (s - 1).inside(B):
                    inverse_std(s - 1)
                if s.inside(B):
                    add_b2(s, lang)
                if (s - 1).inside(B):
                    columns_and_reaction(s - 1)
                if s.inside(B):
                    add_beta(s, lang)

            run_slots(pool, slot, 0, B, 5, B - 2)


def kernel(x, itok_B_0_2, itok_B_0_8, condB_zX, condB_zY, condB_zR, itok_B_0_63, L0_cond_W1, L0_cond_b1, L0_cond_v,
           L1_cond_W1, L1_cond_b1, L1_cond_W2, L1_cond_b2, L1_cond_gamma, L1_cond_beta, L3_cond_W, L3_cond_b):
    import concourse.bacc as bacc
    from concourse.bass_utils import run_bass_kernel_spmd

    def tiles(w):
        w = np.asarray(w)
        *lead, rows, cols = w.shape
        w = np.moveaxis(w.reshape(*lead, rows // P, P, cols), -3, -2)
        return np.ascontiguousarray(w.reshape(*lead, P, rows // P * cols))

    x = np.ascontiguousarray(x)
    L, A, D = L1_cond_W2.shape
    arrays = {
        "x": x,
        "xT": tiles(x.transpose(0, 2, 1)),
        "kinds": np.asarray(itok_B_0_2)[:, None],
        "langs": np.asarray(itok_B_0_8)[:, None],
        "zx": np.asarray(condB_zX)[:, None],
        "zy": np.asarray(condB_zY)[:, None],
        "zr": np.asarray(condB_zR)[:, None],
        "cats": np.asarray(itok_B_0_63)[:, None],
        "w1a": tiles(L0_cond_W1),
        "b1a": np.asarray(L0_cond_b1)[:, None],
        "va": np.asarray(L0_cond_v)[:, None],
        "w1l": tiles(L1_cond_W1),
        "b1l": np.ascontiguousarray(np.asarray(L1_cond_b1).T),
        "w2l": np.ascontiguousarray(np.asarray(L1_cond_W2).transpose(1, 0, 2).reshape(A, L * D)),
        "b2l": np.asarray(L1_cond_b2),
        "gamma": np.asarray(L1_cond_gamma),
        "beta": np.asarray(L1_cond_beta),
        "w3": tiles(L3_cond_W),
        "b3": np.asarray(L3_cond_b),
    }
    arrays = {f"in_{k}": np.ascontiguousarray(v) for k, v in arrays.items()}
    nc = bacc.Bacc("TRN2", target_bir_lowering=False, num_devices=1, dynamic_dma_scratch_size=1024)
    args = [nc.dram_tensor(k, v.shape, mybir.dt.from_np(v.dtype), kind="ExternalInput").ap()
            for k, v in arrays.items()]
    out = nc.dram_tensor("out_x", x.shape, F32, kind="ExternalOutput").ap()
    cond_residual_kernel(nc, *args, out)
    r = run_bass_kernel_spmd(nc, [arrays], core_ids=[0])
    return r.results[0]["out_x"]
```

```python
import numpy as np
import concourse.bass as bass
from concourse import mybir
from contextlib import ExitStack

F32 = mybir.dt.float32
F32R = mybir.dt.float32r
BF16 = mybir.dt.bfloat16
I32 = mybir.dt.int32
ALU = mybir.AluOpType
ACT = mybir.ActivationFunctionType
AX = mybir.AxisListType

P = 128
NEG = -1e30
EPS = 1e-5
UNROLL = 8
CAT, FRESH, WSLOT, LANG, ITEM, KIND, NPARAM = 0, 1, 2, 3, 4, 5, 6
ZX, ZY, ZR = 6, 7, 8
ROW = [(ITEM, 1, -3), (CAT, 1, -1), (ITEM, 1, 3), (CAT, 3, 0), (LANG, 2, 1),
       (WSLOT, 1, -3), (WSLOT, 1, -2), (KIND, 1, 1), (LANG, 1, 0), (CAT + 1, 3, -1)]
W = sum(count for _, count, _ in ROW)
WORDS = {"sp": (0, 8), "pe": (8, 12), "act": (11, 14), "dve": (12, 15), "pool": (11, 14)}
LEAD = 3


class Step:

    def __init__(self, first, turn):
        self.first, self.turn = first, turn

    def __add__(self, k):
        return Step(self.first + k, self.turn)

    def __sub__(self, k):
        return self + (-k)

    def times(self, k):
        return 0 if self.turn is None else self.turn * k

    @property
    def n(self):
        return self.first + self.times(UNROLL)

    def upto(self, back=0):
        return self.first + 1 - back + self.times(UNROLL)

    def dma(self, size=2):
        return 16 * (self.first // size + 1) + self.times(16 * UNROLL // size)

    @property
    def is_first(self):
        return self.turn is None and self.first == 0

    def inside(self, count):
        return self.turn is not None or 0 <= self.first < count

    def ring(self, size):
        return self.first % size

    def is_at_least(self, k):
        return self.first >= k


def run_slots(eng, body, first, last, steady_first, steady_last):
    turns = (steady_last - steady_first + 1) // UNROLL
    for s in range(first, steady_first):
        body(Step(s, None))
    with eng.Fori(0, turns) as turn:
        for j in range(UNROLL):
            body(Step(steady_first + j, turn))
    for s in range(steady_first + turns * UNROLL, last + 1):
        body(Step(s, None))


def cond_residual_kernel(nc, x, xT, kinds, langs, zx, zy, zr, cats, w1a, b1a, va,
                         w1l, b1l, w2l, b2l, gamma, beta, w3, b3, out):
    B, S, D = x.shape
    A = w1a.shape[1] // (D // P)
    K = D // P
    L = gamma.shape[0]
    C = w3.shape[0]
    ctx = ExitStack()

    def sb(name, shape, dt=F32):
        return ctx.enter_context(nc.sbuf_tensor(name, shape, dt))

    def pb(name):
        return ctx.enter_context(nc.psum_tensor(name, [P, 512], F32))

    def sem(name):
        return ctx.enter_context(nc.semaphore(name))

    def ring_sems(name, size=2):
        return [sem(f"{name}{i}") for i in range(size)]

    with ctx:
        b3_parts_dram = nc.dram_tensor("b3_parts_dram", [C, 3, D], BF16, kind="Internal").ap()

        w1_attn = sb("w1_attn", [P, K * A])
        b1_attn = sb("b1_attn", [P, 1])
        v_col = sb("v_col", [P, 1])
        v_wide = sb("v_wide", [P, P])
        w2_all = sb("w2_all", [P, L * D])
        b1_all = sb("b1_all", [P, L])
        b2_wide = sb("b2_wide", [P, L * D])
        gamma_wide = sb("gamma_wide", [P, L * D])
        beta_wide = sb("beta_wide", [P, L * D])
        ident = sb("ident", [P, P])
        ident16 = sb("ident16", [P, P], BF16)
        masks16 = sb("masks16", [P, 3 * P], BF16)
        rows_shift = sb("rows_shift", [P, P])
        rows_shift_r = sb("rows_shift_r", [P, P], F32R)
        mark = {e: sb(f"{e}_mark", [P, 2 * K]) for e in ("act", "dve", "pool")}
        ones3 = sb("ones3", [3, P], BF16)
        iota_row = sb("iota_row", [P, P])
        iota_col = sb("iota_col", [P, 1])
        minus_half = sb("minus_half", [P, 1])
        ones2 = sb("ones2", [P, 2])
        count_t = sb("count_t", [P, B])
        zx_t = sb("zx_t", [P, B])
        zy_t = sb("zy_t", [P, B])
        nzr_t = sb("nzr_t", [P, B])
        c0_t = sb("c0_t", [P, B])
        kind_t = sb("kind_t", [P, B])
        params_by_item = sb("params_by_item", [P, NPARAM], I32)
        all_params = sb("all_params", [1, (B + 2 * LEAD) * W], I32)
        ids_col = sb("ids_col", [P, 3], I32)
        cat_row_i = sb("cat_row_i", [P, B], I32)
        vals = sb("vals", [P, 12])
        rank_col = sb("rank_col", [P, 1])
        key_col = sb("key_col", [P, 1])
        seen_col = sb("seen_col", [P, 1])
        fresh_col = sb("fresh_col", [P, 1])
        slot_i = sb("slot_i", [P, 2], I32)

        xs = sb("xs", [P, 2, D])
        xts = sb("xts", [P, 2, K, S])
        w1s = sb("w1s", [P, 2, K, A])
        w3s = sb("w3s", [P, 2 * K * D])
        w3_hi = sb("w3_hi", [P, 2 * K * D], F32R)
        w3_lo = sb("w3_lo", [P, 2 * K * D], F32R)
        b3s = sb("b3s", [3, 2, D], BF16)
        cat_row, key_row, less, same, place, tmp = (w3s[:, i * P:(i + 1) * P] for i in range(6))
        wide = w3s[:, 6 * P:10 * P]
        b3_f, b3_rest = w3s[0:C, 10 * P:10 * P + D], w3s[0:C, 10 * P + D:10 * P + 2 * D]
        b3_parts = w3s[0:C, 10 * P + 2 * D:10 * P + 4 * D].bitcast(BF16)
        attn = sb("attn", [P, 2, S])
        neg_max = sb("neg_max", [P, 2])
        probs = sb("probs", [P, 2, S])
        prob_sum = sb("prob_sum", [P, 2])
        denom = sb("denom", [P, 2])
        scale = sb("scale", [P, 2])
        probsT = sb("probsT", [P, 2, S])
        x1 = sb("x1", [P, 2, D])
        x1T = sb("x1T", [P, 2, D])
        x1_b2 = sb("x1_b2", [P, D])
        x1_beta = sb("x1_beta", [P, 2, D])
        hid = sb("hid", [P, 2, S])
        y = sb("y", [P, 2, D])
        y_sum = sb("y_sum", [P, 2])
        neg_mean = sb("neg_mean", [P, 2])
        square_junk = sb("square_junk", [P, D])
        var_sum = sb("var_sum", [P, 2])
        var_eps = sb("var_eps", [P, 2])
        rstd = sb("rstd", [P, 2])
        x2 = sb("x2", [P, 2, D + 2])
        react = sb("react", [P, D])
        neighbours = sb("neighbours", [P, D])
        x2_hi = sb("x2_hi", [P, 2, D], F32R)
        x2_lo = sb("x2_lo", [P, 2, D], F32R)
        x3 = sb("x3", [P, 2, D])
        x3T_hi = sb("x3T_hi", [P, 2, D], F32R)
        x3T_lo = sb("x3T_lo", [P, 2, D], F32R)
        res = sb("res", [P, 2, D])

        bank_hidden = pb("bank_hidden")
        ps_attn, ps_hid = bank_hidden[:, 0:S], bank_hidden[:, S:2 * S]
        bank_scores = pb("bank_scores")
        ps_scores, ps_probsT = bank_scores[:, 0:S], bank_scores[:, S:2 * S]
        ps_pool = pb("ps_pool")
        ps_x1T = ps_pool
        ps_x3T = pb("ps_x3T")
        ps_adapt = pb("ps_adapt")
        ps_rows = pb("ps_rows")
        ps_out = [pb("ps_out0"), pb("ps_out1")]

        tables_in = sem("tables_in")
        w2_in, b2_in, beta_in, gamma_in = sem("w2_in"), sem("b2_in"), sem("beta_in"), sem("gamma_in")
        ids_in = sem("ids_in")
        b3_in = sem("b3_in")
        b3_parts_out = sem("b3_parts_out")
        params_in = sem("params_in")
        PARAMS_IN = 16 * len(ROW)
        x_in, xT_in, w1_in = ring_sems("x_in"), ring_sems("xT_in"), ring_sems("w1_in")
        w3_in, b3row_in, res_out = ring_sems("w3_in"), ring_sems("b3row_in"), ring_sems("res_out")
        consts_made = sem("consts_made")
        prep = sem("prep")
        pool_prep = sem("pool_prep")
        params_zeroed = sem("params_zeroed")
        b3_split = sem("b3_split")
        fresh_made, slots_summed = sem("fresh_made"), sem("slots_summed")
        place_made, sorted_made, tables_made = sem("place_made"), sem("sorted_made"), sem("tables_made")
        params_made = sem("params_made")
        gconst = sem("gconst")
        attn_mm, scores_mm, probsT_mm, pool_mm = (sem(n) for n in ("attn_mm", "scores_mm", "probsT_mm", "pool_mm"))
        x1T_mm, hid_mm, adapt_mm, rows_mm, x3T_mm, out_mm = (
            sem(n) for n in ("x1T_mm", "hid_mm", "adapt_mm", "rows_mm", "x3T_mm", "out_mm"))
        attn_ready, probs_ready, probsT_ready, x1T_ready, var_ready, react_ready, x3T_hi_ready = (
            sem(n) for n in ("attn_ready", "probs_ready", "probsT_ready", "x1T_ready", "var_ready",
                             "react_ready", "x3T_hi_ready"))
        relu_ready, x2_hi_ready, w3_hi_ready = sem("relu_ready"), sem("x2_hi_ready"), sem("w3_hi_ready")
        x3T_lo_ready, x2_lo_ready, w3_lo_ready = sem("x3T_lo_ready"), sem("x2_lo_ready"), sem("w3_lo_ready")
        w3_lo_end_ready = sem("w3_lo_end_ready")
        max_ready, denom_ready, scale_ready, x1_ready, y_ready, mean_ready, norm_ready = (
            sem(n) for n in ("max_ready", "denom_ready", "scale_ready", "x1_ready", "y_ready",
                             "mean_ready", "norm_ready"))
        x2_ready, partial_ready, x3_ready, res_ready = (
            sem(n) for n in ("x2_ready", "partial_ready", "x3_ready", "res_ready"))
        edges_ready, neighbours_ready, react_x2_ready, x1_b2_ready, x1_beta_ready = (
            sem(n) for n in ("edges_ready", "neighbours_ready", "react_x2_ready", "x1_b2_ready",
                             "x1_beta_ready"))
        vareps_ready, rstd_ready = sem("vareps_ready"), sem("rstd_ready")

        block = ctx.enter_context(nc.Block())

        tops = {ITEM: B - 1, CAT: C - 1, LANG: L - 1, KIND: 2, FRESH: 1, WSLOT: 1}

        def load_params(eng, name, s):
            why = "the ids index the tables' rows, the rest is made here"
            first, last = WORDS[name]
            whats = [what + i for what, count, _ in ROW for i in range(count)][first:last]
            _, values = nc.values_load_multi_w_load_instructions(
                all_params[:, bass.ds((s + LEAD).n * W + first, last - first)], engines=[eng.engine],
                min_val=0, max_val=B - 1, skip_runtime_bounds_check_because=why)
            return [nc.s_assert_within(v, 0, tops[what], skip_runtime_bounds_check_because=why)
                    for v, what in zip(values, whats)]

        @block.sync
        def _(sp):
            sp.dma_start(ids_col[:, 0:1], cats).then_inc(ids_in, 16)
            sp.dma_start(ids_col[:, 1:2], langs).then_inc(ids_in, 16)
            sp.dma_start(ids_col[:, 2:3], kinds).then_inc(ids_in, 16)
            sp.dma_start(vals[:, ZX:ZX + 1], zx).then_inc(ids_in, 16)
            sp.dma_start(vals[:, ZY:ZY + 1], zy).then_inc(ids_in, 16)
            sp.dma_start(vals[:, ZR:ZR + 1], zr).then_inc(ids_in, 16)
            sp.dma_start(cat_row_i[:, :], cats.rearrange("b o -> (o b)").partition_broadcast(P)).then_inc(ids_in, 16)
            sp.dma_start(v_col[:, :], va).then_inc(ids_in, 16)
            sp.dma_start(b3_f[:, :], b3).then_inc(b3_in, 16)
            sp.dma_start(w1_attn[:, :], w1a).then_inc(tables_in, 16)
            sp.dma_start(b1_attn[:, :], b1a).then_inc(tables_in, 16)
            sp.dma_start(b1_all[:, :], b1l).then_inc(tables_in, 16)
            sp.dma_start(w2_all[:, :], w2l).then_inc(w2_in, 16)

            def load_wide(table, src, loaded, langs=slice(0, L)):
                sp.dma_start(table[:, langs.start * D:langs.stop * D],
                             src[langs].rearrange("l d -> (l d)").partition_broadcast(P)).then_inc(loaded, 16)

            load_wide(b2_wide, b2l, b2_in, slice(0, L // 2))
            sp.wait_ge(params_made, 1)
            sp.wait_ge(params_zeroed, 1)
            table, k = all_params.rearrange("o (r w) -> o r w", w=W), 0
            with nc.allow_non_contiguous_dma(reason="a few hundred words, once"):
                for what, count, ahead in ROW:
                    sp.dma_start(table[:, LEAD - ahead:LEAD - ahead + B, k:k + count],
                                 params_by_item[:, what:what + count]).then_inc(params_in, 16)
                    k += count
            sp.wait_ge(b3_split, 1)
            sp.dma_start(b3_parts_dram, b3_parts[:, 0:3 * D].rearrange("c (t d) -> c t d", t=3)
                         ).then_inc(b3_parts_out, 16)
            sp.wait_ge(params_in, PARAMS_IN)

            def load_xT(a, item):
                r = a.ring(2)
                if a.is_at_least(2):
                    sp.wait_ge(attn_mm, a.upto(2))
                sp.dma_start(xts[:, r], xT[bass.ds(item, 1)].rearrange("o p (k s) -> p (o k) s", k=K)
                             ).then_inc(xT_in[r], 16)

            def load_x(a, item, lang):
                r = a.ring(2)
                if a.is_at_least(2):
                    sp.wait_ge(x1_ready, a.upto(2))
                sp.dma_start(xs[:, r], x[bass.ds(item, 1)].rearrange("o s d -> s (o d)")).then_inc(x_in[r], 16)
                if a.is_at_least(2):
                    sp.wait_ge(hid_mm, a.upto(2))
                sp.dma_start(w1s[:, r], w1l[bass.ds(lang, 1)].rearrange("o p (k a) -> p (o k) a", k=K)
                             ).then_inc(w1_in[r], 16)

            def load_w3(c, cat, fresh, wslot):
                r = c.ring(2)
                if c.is_first:
                    sp.wait_ge(tables_made, 1)
                    sp.wait_ge(b3_parts_out, 16)
                if c.is_at_least(2):
                    sp.wait_ge(w3_hi_ready, c.upto(2) * K)
                    sp.wait_ge(w3_lo_end_ready, c.upto(2))
                sp.dma_start(w3s[:, bass.ds(wslot * (K * D), K * D)],
                             w3[bass.ds(cat, 1)].rearrange("o p n -> p (o n)"),
                             cond=fresh, bounds_check="skip_entire_dma").then_inc(w3_in[r], 16)

            def load_b3(c, cat):
                r = c.ring(2)
                if c.is_at_least(2):
                    sp.wait_ge(out_mm, c.upto(2))
                sp.dma_start(b3s[:, r], b3_parts_dram[bass.ds(cat, 1)].rearrange("o t d -> t (o d)")
                             ).then_inc(b3row_in[r], 16)

            def store(o, item):
                sp.wait_ge(res_ready, o.upto())
                sp.dma_start(out[bass.ds(item, 1)].rearrange("o s d -> s (o d)"), res[:, o.ring(2)]
                             ).then_inc(res_out[o.ring(2)], 16)

            def slot(s):
                item_m3, cat_m1, item_p3, cat, fresh, wslot, lang_p1, item_p1 = load_params(sp, "sp", s)
                if (s + 3).inside(B):
                    load_xT(s + 3, item_p3)
                if (s + 1).inside(B):
                    load_x(s + 1, item_p1, lang_p1)
                if s.inside(B):
                    load_w3(s, cat, fresh, wslot)
                if (s - 1).inside(B):
                    load_b3(s - 1, cat_m1)
                if (s - 3).inside(B):
                    store(s - 3, item_m3)
                if s.turn is None and s.first in late_tables:
                    load_wide(*late_tables[s.first])

            late_tables = {-2: (b2_wide, b2l, b2_in, slice(L // 2, L)), -1: (beta_wide, beta, beta_in),
                           0: (gamma_wide, gamma, gamma_in)}

            run_slots(sp, slot, -3, B + 2, 5, B - 4)
            for r in range(2):
                sp.wait_ge(res_out[r], 16 * (B // 2))
                sp.wait_ge(w3_in[r], 16 * (B // 2))

        @block.tensor
        def _(pe):
            pe.wait_ge(fresh_made, 1)
            pe.matmul(ps_pool[:, 0:1], less[:, :], fresh_col[:, :], start=True, stop=True).then_inc(slots_summed, 1)
            pe.wait_ge(place_made, 1)
            pe.matmul(ps_adapt[:, 0:NPARAM], place[:, :], vals[:, 0:NPARAM], start=True, stop=True
                      ).then_inc(sorted_made, 1)
            for i in range(4):
                mm = pe.matmul(ps_rows[:, i * P:(i + 1) * P], wide[:, i * P:(i + 1) * P], place[:, :],
                               start=True, stop=True)
            mm.then_inc(sorted_made, 1)
            pe.wait_ge(tables_made, 1)
            pe.wait_ge(gconst, 1)
            pe.wait_ge(tables_in, 16 * 3)
            pe.wait_ge(params_in, PARAMS_IN)

            def attn_project(a):
                r = a.ring(2)
                pe.wait_ge(xT_in[r], a.dma())
                if a.is_at_least(1):
                    pe.wait_ge(attn_ready, a.upto(1))
                if a.is_at_least(3):
                    pe.wait_ge(relu_ready, a.upto(3))
                for k in range(K):
                    mm = pe.matmul(ps_attn, w1_attn[:, k * A:(k + 1) * A], xts[:, r, k, :],
                                   start=(k == 0), stop=(k == K - 1))
                mm.then_inc(attn_mm, 1)

            def attn_scores(b, kind):
                pe.wait_ge(attn_ready, b.upto())
                if b.is_at_least(1):
                    pe.wait_ge(probsT_ready, b.upto(1))
                pe.matmul(ps_scores, v_wide[:, :], attn[:, b.ring(2), :], start=True, stop=False)
                pe.matmul(ps_scores, ident16[:, :], masks16[:, bass.ds(kind * P, P)], start=False, stop=True
                          ).then_inc(scores_mm, 1)

            def probs_transpose(c):
                pe.wait_ge(probs_ready, c.upto())
                pe.transpose(ps_probsT, probs[:, c.ring(2), :], ident[:, :]).then_inc(probsT_mm, 1)

            def pool(d):
                pe.wait_ge(probsT_ready, d.upto())
                pe.wait_ge(x_in[d.ring(2)], d.dma())
                if d.is_at_least(1):
                    pe.wait_ge(x1T_ready, d.upto(1))
                pe.matmul(ps_pool[:, :], probsT[:, d.ring(2), :], xs[:, d.ring(2), :], start=True, stop=True
                          ).then_inc(pool_mm, 1)

            def x1_transpose(e):
                pe.wait_ge(x1_ready, e.upto())
                for k in range(K):
                    mm = pe.transpose(ps_x1T[:, k * P:(k + 1) * P], x1[:, e.ring(2), k * P:(k + 1) * P], ident[:, :])
                mm.then_inc(x1T_mm, 1)

            def x3_transpose(i):
                pe.wait_ge(x3_ready, i.upto())
                if i.is_at_least(1):
                    pe.wait_ge(x3T_lo_ready, i.upto(1))
                for k in range(K):
                    mm = pe.transpose(ps_x3T[:, k * P:(k + 1) * P], x3[:, i.ring(2), k * P:(k + 1) * P], ident[:, :])
                mm.then_inc(x3T_mm, 1)

            def adapter_down(f):
                pe.wait_ge(x1T_ready, f.upto())
                pe.wait_ge(w1_in[f.ring(2)], f.dma())
                if f.is_at_least(1):
                    pe.wait_ge(relu_ready, f.upto(1))
                if (f + 2).inside(B):
                    pe.wait_ge(attn_ready, (f + 2).upto())
                for k in range(K):
                    mm = pe.matmul(ps_hid, w1s[:, f.ring(2), k, :], x1T[:, f.ring(2), k * P:(k + 1) * P],
                                   start=(k == 0), stop=(k == K - 1))
                mm.then_inc(hid_mm, 1)

            def adapter_up(g, lang):
                pe.wait_ge(relu_ready, g.upto())
                if g.is_first:
                    pe.wait_ge(w2_in, 16)
                if g.is_at_least(1):
                    pe.wait_ge(y_ready, g.upto(1))
                pe.matmul(ps_adapt[:, :], hid[:, g.ring(2), :], w2_all[:, bass.ds(lang * D, D)],
                          start=True, stop=True).then_inc(adapt_mm, 1)

            def rows_laplacian(h):
                pe.wait_ge(x2_hi_ready, h.upto())
                pe.wait_ge(x2_lo_ready, h.upto())
                if h.is_at_least(1):
                    pe.wait_ge(partial_ready, h.upto(1))
                pe.matmul(ps_rows[:, :], rows_shift_r[:, :], x2_hi[:, h.ring(2), :], start=True, stop=False)
                pe.matmul(ps_rows[:, :], rows_shift_r[:, :], x2_lo[:, h.ring(2), :], start=False, stop=True
                          ).then_inc(rows_mm, 1)

            def category_bias(j):
                pe.wait_ge(b3row_in[j.ring(2)], j.dma())
                if j.is_at_least(2):
                    pe.wait_ge(res_ready, j.upto(2))
                pe.matmul(ps_out[j.ring(2)][:, :], ones3[:, :], b3s[:, j.ring(2), :], start=True, stop=False)

            def category_high(j, wslot):
                pe.wait_ge(x3T_hi_ready, j.upto())
                pe.wait_ge(w3_hi_ready, j.upto() * K)
                pe.wait_ge(w3_lo_end_ready, j.upto())
                for k in range(K):
                    for part in (w3_hi, w3_lo):
                        pe.matmul(ps_out[j.ring(2)][:, :], x3T_hi[:, j.ring(2), k * P:(k + 1) * P],
                                  part[:, bass.ds(wslot * (K * D) + k * D, D)], start=False, stop=False)

            def category_low(j, wslot, ks):
                if 0 in ks:
                    pe.wait_ge(x3T_lo_ready, j.upto())
                for k in ks:
                    mm = pe.matmul(ps_out[j.ring(2)][:, :], x3T_lo[:, j.ring(2), k * P:(k + 1) * P],
                                   w3_hi[:, bass.ds(wslot * (K * D) + k * D, D)], start=False, stop=(k == K - 1))
                if K - 1 in ks:
                    mm.then_inc(out_mm, 1)

            def slot(s):
                j = s - 2
                if s.inside(B):
                    pool(s)
                if (s + 2).inside(B):
                    attn_project(s + 2)
                last_wslot, wslot, kind, lang = load_params(pe, "pe", s)
                if (s + 1).inside(B):
                    attn_scores(s + 1, kind)
                if (j - 1).inside(B):
                    category_low(j - 1, last_wslot, range(0, K // 2))
                if s.inside(B):
                    x1_transpose(s)
                if (j - 1).inside(B):
                    category_low(j - 1, last_wslot, range(K // 2, K))
                if j.inside(B):
                    x3_transpose(j)
                    category_bias(j)
                if s.inside(B):
                    adapter_down(s)
                if (s + 1).inside(B):
                    probs_transpose(s + 1)
                if j.inside(B):
                    category_high(j, wslot)
                if (s - 1).inside(B):
                    rows_laplacian(s - 1)
                if s.inside(B):
                    adapter_up(s, lang)

            run_slots(pe, slot, -2, B + 2, 6, B - 3)

        @block.scalar
        def _(act):
            act.wait_ge(tables_made, 1)
            act.wait_ge(tables_in, 16 * 3)

            def high_x3T(i):
                act.wait_ge(x3T_mm, i.upto())
                if i.is_at_least(2):
                    act.wait_ge(out_mm, i.upto(2))
                nc.scalar.activation(x3T_hi[:, i.ring(2), :], ps_x3T[:, :], ACT.Copy).then_inc(x3T_hi_ready, 1)

            def variance(h):
                q = h.ring(2)
                act.wait_ge(mean_ready, h.upto())
                if h.is_at_least(2):
                    act.wait_ge(vareps_ready, h.upto(2))
                nc.scalar.activation(square_junk[:, :], y[:, q, :], ACT.Square, bias=neg_mean[:, q:q + 1],
                                     accum_out=var_sum[:, q:q + 1]).then_inc(var_ready, 1)

            def high_x2(h):
                act.wait_ge(x2_ready, h.upto())
                if h.is_at_least(2):
                    act.wait_ge(rows_mm, h.upto(2))
                nc.scalar.activation(x2_hi[:, h.ring(2), :], x2[:, h.ring(2), 1:D + 1], ACT.Copy
                                     ).then_inc(x2_hi_ready, 1)

            def reaction(h):
                if h.is_at_least(1):
                    act.wait_ge(x3_ready, h.upto(1))
                nc.scalar.activation(react[:, :], x2[:, h.ring(2), 1:D + 1], ACT.Identity,
                                     bias=c0_t[:, bass.ds(h.n, 1)], scale=nzr_t[:, bass.ds(h.n, 1)]
                                     ).then_inc(react_ready, 1)

            def move_x1T(s):
                act.wait_ge(x1T_mm, s.upto())
                if s.is_at_least(2):
                    act.wait_ge(hid_mm, s.upto(2))
                nc.scalar.activation(x1T[:, s.ring(2), :], ps_x1T[:, :], ACT.Copy).then_inc(x1T_ready, 1)

            def attn_tanh(a):
                act.wait_ge(attn_mm, a.upto())
                if a.is_at_least(2):
                    act.wait_ge(scores_mm, a.upto(2))
                nc.scalar.activation(attn[:, a.ring(2), :], ps_attn, ACT.Tanh, bias=b1_attn[:, 0:1]
                                     ).then_inc(attn_ready, 1)

            def exponentials(b):
                act.wait_ge(max_ready, b.upto())
                if b.is_at_least(2):
                    act.wait_ge(probsT_mm, b.upto(2))
                    act.wait_ge(denom_ready, b.upto(2))
                nc.scalar.activation(probs[:, b.ring(2), :], ps_scores, ACT.Exp,
                                     bias=neg_max[:, b.ring(2):b.ring(2) + 1],
                                     accum_out=prob_sum[:, b.ring(2):b.ring(2) + 1]).then_inc(probs_ready, 1)

            def move_probsT(b):
                act.wait_ge(probsT_mm, b.upto())
                if b.is_at_least(2):
                    act.wait_ge(pool_mm, b.upto(2))
                nc.scalar.activation(probsT[:, b.ring(2), :], ps_probsT, ACT.Copy).then_inc(probsT_ready, 1)

            def relu(f, lang):
                act.wait_ge(hid_mm, f.upto())
                if f.is_at_least(2):
                    act.wait_ge(adapt_mm, f.upto(2))
                nc.scalar.activation(hid[:, f.ring(2), :], ps_hid, ACT.Relu, bias=b1_all[:, bass.ds(lang, 1)]
                                     ).then_inc(relu_ready, 1)

            def high_w3(c, fresh, wslot, ks):
                with act.If(fresh):
                    if 0 in ks:
                        act.wait_ge(w3_in[c.ring(2)], c.dma())
                        if c.is_at_least(2):
                            act.wait_ge(out_mm, c.upto(2))
                    for k in ks:
                        piece = bass.ds(wslot * (K * D) + k * D, D)
                        nc.scalar.activation(w3_hi[:, piece], w3s[:, piece], ACT.Copy).then_inc(w3_hi_ready, 1)
                with act.Else():
                    column = slice(c.ring(2) * K + ks[0], c.ring(2) * K + ks[0] + 1)
                    nc.scalar.activation(mark["act"][:, column], b1_attn[:, :], ACT.Copy
                                         ).then_inc(w3_hi_ready, len(ks))

            def slot(s):
                c = s - 1
                if c.inside(B):
                    variance(s - 1)
                if (s + 2).inside(B):
                    attn_tanh(s + 2)
                lang, fresh, wslot = load_params(act, "act", s)
                if s.inside(B):
                    move_x1T(s)
                if (s + 1).inside(B):
                    exponentials(s + 1)
                if (s - 2).inside(B):
                    high_x3T(s - 2)
                if c.inside(B):
                    high_w3(c, fresh, wslot, [0])
                    high_x2(s - 1)
                    high_w3(c, fresh, wslot, [1])
                    reaction(s - 1)
                if s.inside(B):
                    relu(s, lang)
                if c.inside(B):
                    high_w3(c, fresh, wslot, [2])
                if (s + 1).inside(B):
                    move_probsT(s + 1)
                if c.inside(B):
                    high_w3(c, fresh, wslot, [3])

            run_slots(act, slot, -2, B + 1, 6, B - 3)

        @block.vector
        def _(dve):
            steps = [0]

            def then(ins):
                steps[0] += 1
                ins.then_inc(prep, 1)
                dve.wait_ge(prep, steps[0])

            dve.wait_ge(ids_in, 16 * 8)
            dve.wait_ge(consts_made, 1)
            nc.vector.memset(ones3[:, :], 1.0)
            nc.vector.memset(minus_half[:, :], -0.5)
            nc.vector.memset(ones2[:, :], 1.0)
            nc.vector.tensor_copy(vals[:, ITEM:ITEM + 1], iota_col[:, :])
            for i, what in enumerate((CAT, LANG, KIND)):
                nc.vector.tensor_copy(vals[:, what:what + 1], ids_col[:, i:i + 1])
            nc.vector.tensor_copy(ident16[:, :], ident[:, :])
            then(nc.vector.tensor_copy(cat_row[:, :], cat_row_i[:, :]))
            nc.vector.scalar_tensor_tensor(key_row[:, :], cat_row[:, :], float(B), iota_row[:, :], ALU.mult, ALU.add)
            then(nc.vector.scalar_tensor_tensor(key_col[:, :], vals[:, CAT:CAT + 1], float(B), iota_col[:, :],
                                                ALU.mult, ALU.add))
            then(nc.vector.tensor_scalar(less[:, :], key_row[:, :], key_col[:, 0:1], None, ALU.is_lt))
            nc.vector.tensor_reduce(rank_col[:, :], less[:, :], AX.X, ALU.add)
            then(nc.vector.tensor_scalar(same[:, :], cat_row[:, :], vals[:, CAT:CAT + 1], None, ALU.is_equal))
            then(nc.vector.tensor_tensor(same[:, :], same[:, :], less[:, :], ALU.mult))
            then(nc.vector.tensor_reduce(seen_col[:, :], same[:, :], AX.X, ALU.add))
            nc.vector.tensor_scalar(fresh_col[:, :], seen_col[:, :], 0.0, None, ALU.is_equal)
            then(nc.vector.tensor_scalar(less[:, :], cat_row[:, :], vals[:, CAT:CAT + 1], None, ALU.is_gt))
            for i, what in enumerate((ZX, ZY, ZR, KIND)):
                nc.vector.tensor_scalar(wide[:, i * P:(i + 1) * P], ident[:, :], 0.0, vals[:, what:what + 1],
                                        ALU.mult, ALU.add)
            nc.vector.tensor_scalar(v_wide[:, :], ident[:, :], 0.0, v_col[:, 0:1], ALU.mult, ALU.add)
            nc.vector.tensor_copy(vals[:, FRESH:FRESH + 1], fresh_col[:, :]).then_inc(fresh_made, 1)
            dve.wait_ge(slots_summed, 1)
            then(nc.vector.tensor_copy(slot_i[:, 0:1], ps_pool[:, 0:1]))
            then(nc.vector.tensor_scalar(slot_i[:, 1:2], slot_i[:, 0:1], 1, None, ALU.bitwise_and))
            nc.vector.tensor_copy(vals[:, WSLOT:WSLOT + 1], slot_i[:, 1:2])
            nc.vector.tensor_scalar(place[:, :], iota_row[:, :], rank_col[:, 0:1], None, ALU.is_equal
                                    ).then_inc(place_made, 1)
            dve.wait_ge(sorted_made, 1)
            nc.vector.tensor_copy(params_by_item[:, :], ps_adapt[:, 0:NPARAM]).then_inc(params_made, 1)
            dve.wait_ge(b3_in, 16)
            then(nc.vector.tensor_copy(b3_parts[:, 0:D], b3_f[:, :]))
            then(nc.vector.tensor_tensor(b3_rest[:, :], b3_f[:, :], b3_parts[:, 0:D], ALU.subtract))
            then(nc.vector.tensor_copy(b3_parts[:, D:2 * D], b3_rest[:, :]))
            then(nc.vector.tensor_tensor(b3_rest[:, :], b3_rest[:, :], b3_parts[:, D:2 * D], ALU.subtract))
            nc.vector.tensor_copy(b3_parts[:, 2 * D:3 * D], b3_rest[:, :]).then_inc(b3_split, 1)
            dve.wait_ge(sorted_made, 2)
            nc.vector.tensor_copy(zx_t[:, :], ps_rows[:, 0:P])
            nc.vector.tensor_copy(zy_t[:, :], ps_rows[:, P:2 * P])
            nc.vector.tensor_scalar(nzr_t[:, :], ps_rows[:, 2 * P:3 * P], -1.0, None, ALU.mult)
            then(nc.vector.tensor_copy(kind_t[:, :], ps_rows[:, 3 * P:4 * P]))
            then(nc.vector.tensor_tensor(tmp[:, :], zx_t[:, :], zy_t[:, :], ALU.add))
            then(nc.vector.tensor_scalar(tmp[:, :], tmp[:, :], -2.0, 1.0, ALU.mult, ALU.add))
            then(nc.vector.tensor_tensor(c0_t[:, :], tmp[:, :], nzr_t[:, :], ALU.subtract))
            nc.vector.tensor_scalar(key_col[:, :], iota_col[:, :], 1.0, None, ALU.add)
            nc.vector.tensor_scalar(seen_col[:, :], iota_col[:, :], -1.0, float(S), ALU.mult, ALU.add)
            then(nc.vector.tensor_scalar(tmp[:, :], kind_t[:, :], 0.0, None, ALU.is_equal))
            then(nc.vector.tensor_scalar(count_t[:, :], tmp[:, :], key_col[:, 0:1], None, ALU.mult))
            then(nc.vector.tensor_scalar(tmp[:, :], kind_t[:, :], 1.0, None, ALU.is_equal))
            then(nc.vector.scalar_tensor_tensor(count_t[:, :], tmp[:, :], seen_col[:, 0:1], count_t[:, :],
                                                ALU.mult, ALU.add))
            then(nc.vector.tensor_scalar(tmp[:, :], kind_t[:, :], 1.5, float(S - 1), ALU.is_gt, ALU.mult))
            then(nc.vector.tensor_tensor(count_t[:, :], count_t[:, :], tmp[:, :], ALU.add))
            dve.wait_ge(gconst, 1)
            nc.vector.tensor_copy(rows_shift_r[:, :], rows_shift[:, :])
            dve.wait_ge(b3_split, 1)
            nc.vector.memset(mark["dve"][:, :], 0.0).then_inc(tables_made, 1)
            dve.wait_ge(tables_in, 16 * 3)
            dve.wait_ge(params_in, PARAMS_IN)

            def add_adapted(h):
                q = h.ring(2)
                dve.wait_ge(adapt_mm, h.upto())
                dve.wait_ge(x1_b2_ready, h.upto())
                nc.vector.scalar_tensor_tensor(y[:, q, :], ps_adapt[:, :], 1.0, x1_b2[:, :], ALU.mult, ALU.add,
                                               accum_out=y_sum[:, q:q + 1]).then_inc(y_ready, 1)
                dve.wait_ge(y_ready, h.upto())
                nc.vector.tensor_scalar(neg_mean[:, q:q + 1], y_sum[:, q:q + 1], -1.0 / D, None, ALU.mult
                                        ).then_inc(mean_ready, 1)

            def add_pooled(s):
                q = s.ring(2)
                dve.wait_ge(pool_mm, s.upto())
                dve.wait_ge(scale_ready, s.upto())
                if s.is_at_least(2):
                    dve.wait_ge(x1T_mm, s.upto(2))
                    dve.wait_ge(x1_beta_ready, s.upto(2))
                    dve.wait_ge(x1_b2_ready, s.upto(2))
                nc.vector.scalar_tensor_tensor(x1[:, q, :], ps_pool[:, :], scale[:, q:q + 1], xs[:, s.ring(2), :],
                                               ALU.mult, ALU.add).then_inc(x1_ready, 1)

            def result(o):
                dve.wait_ge(out_mm, o.upto())
                if o.is_at_least(2):
                    dve.wait_ge(res_out[o.ring(2)], (o - 2).dma())
                nc.vector.tensor_tensor(res[:, o.ring(2), :], ps_out[o.ring(2)][:, :], x3[:, o.ring(2), :], ALU.add
                                        ).then_inc(res_ready, 1)

            def low_x3T(i):
                dve.wait_ge(x3T_hi_ready, i.upto())
                if i.is_at_least(2):
                    dve.wait_ge(out_mm, i.upto(2))
                nc.vector.tensor_tensor(x3T_lo[:, i.ring(2), :], ps_x3T[:, :], x3T_hi[:, i.ring(2), :].bitcast(F32),
                                        ALU.subtract).then_inc(x3T_lo_ready, 1)

            def add_epsilon(h):
                q = h.ring(2)
                dve.wait_ge(var_ready, h.upto())
                if h.is_at_least(2):
                    dve.wait_ge(rstd_ready, h.upto(2))
                nc.vector.tensor_scalar(var_eps[:, q:q + 1], var_sum[:, q:q + 1], 1.0 / D, EPS,
                                        ALU.mult, ALU.add).then_inc(vareps_ready, 1)

            def center(h, lang):
                q = h.ring(2)
                if h.is_first:
                    dve.wait_ge(gamma_in, 16)
                nc.vector.scalar_tensor_tensor(y[:, q, :], y[:, q, :], neg_mean[:, q:q + 1],
                                               gamma_wide[:, bass.ds(lang * D, D)], ALU.add, ALU.mult
                                               ).then_inc(norm_ready, 1)

            def normalize(h):
                q = h.ring(2)
                dve.wait_ge(norm_ready, h.upto())
                dve.wait_ge(rstd_ready, h.upto())
                dve.wait_ge(x1_beta_ready, h.upto())
                if h.is_at_least(2):
                    dve.wait_ge(react_ready, h.upto(2))
                    dve.wait_ge(react_x2_ready, h.upto(2))
                    dve.wait_ge(neighbours_ready, h.upto(2))
                nc.vector.scalar_tensor_tensor(x2[:, q, 1:D + 1], y[:, q, :], rstd[:, q:q + 1], x1_beta[:, q, :],
                                               ALU.mult, ALU.add).then_inc(x2_ready, 1)

            def low_x2(h):
                q = h.ring(2)
                dve.wait_ge(x2_hi_ready, h.upto())
                if h.is_at_least(2):
                    dve.wait_ge(rows_mm, h.upto(2))
                nc.vector.tensor_tensor(x2_lo[:, q, :], x2[:, q, 1:D + 1], x2_hi[:, q, :].bitcast(F32), ALU.subtract
                                        ).then_inc(x2_lo_ready, 1)

            def low_w3(c, fresh, wslot):
                with dve.If(fresh):
                    if c.is_at_least(2):
                        dve.wait_ge(out_mm, c.upto(2))
                    for k in range(K - 1):
                        dve.wait_ge(w3_hi_ready, c.upto() * K - (K - 1 - k))
                        piece = bass.ds(wslot * (K * D) + k * D, D)
                        nc.vector.tensor_tensor(w3_lo[:, piece], w3s[:, piece], w3_hi[:, piece].bitcast(F32),
                                                ALU.subtract).then_inc(w3_lo_ready, 1)
                with dve.Else():
                    nc.vector.memset(mark["dve"][:, c.ring(2):c.ring(2) + 1], 0.0).then_inc(w3_lo_ready, K - 1)

            def row_max(b):
                p = b.ring(2)
                dve.wait_ge(scores_mm, b.upto())
                if b.is_at_least(2):
                    dve.wait_ge(probs_ready, b.upto(2))
                nc.vector.tensor_reduce(neg_max[:, p:p + 1], ps_scores, AX.X, ALU.max, negate=True
                                        ).then_inc(max_ready, 1)

            def denominator(b):
                p = b.ring(2)
                dve.wait_ge(probs_ready, b.upto())
                nc.vector.tensor_tensor(denom[:, p:p + 1], prob_sum[:, p:p + 1], count_t[:, bass.ds(b.n, 1)],
                                        ALU.mult).then_inc(denom_ready, 1)

            def row_scale(b):
                p = b.ring(2)
                dve.wait_ge(denom_ready, b.upto())
                nc.vector.reciprocal(scale[:, p:p + 1], denom[:, p:p + 1]).then_inc(scale_ready, 1)

            def add_rows(h):
                dve.wait_ge(rows_mm, h.upto())
                dve.wait_ge(react_x2_ready, h.upto())
                nc.vector.scalar_tensor_tensor(react[:, :], ps_rows[:, :], zy_t[:, bass.ds(h.n, 1)], react[:, :],
                                               ALU.mult, ALU.add).then_inc(partial_ready, 1)

            def add_columns(h):
                dve.wait_ge(partial_ready, h.upto())
                dve.wait_ge(neighbours_ready, h.upto())
                if h.is_at_least(2):
                    dve.wait_ge(x3T_mm, h.upto(2))
                nc.vector.scalar_tensor_tensor(x3[:, h.ring(2), :], neighbours[:, :], zx_t[:, bass.ds(h.n, 1)],
                                               react[:, :], ALU.mult, ALU.add).then_inc(x3_ready, 1)

            def slot(s):
                c = s - 1
                if c.inside(B):
                    add_adapted(s - 1)
                if s.inside(B):
                    add_pooled(s)
                if (s - 2).inside(B):
                    add_columns(s - 2)
                fresh, wslot, lang = load_params(dve, "dve", s)
                if c.inside(B):
                    add_epsilon(s - 1)
                if (s + 1).inside(B):
                    row_max(s + 1)
                if c.inside(B):
                    center(s - 1, lang)
                    normalize(s - 1)
                if (s - 3).inside(B):
                    result(s - 3)
                if (s - 2).inside(B):
                    low_x3T(s - 2)
                if (s + 1).inside(B):
                    denominator(s + 1)
                if c.inside(B):
                    low_x2(s - 1)
                if (s + 1).inside(B):
                    row_scale(s + 1)
                if c.inside(B):
                    low_w3(c, fresh, wslot)
                    add_rows(s - 1)

            run_slots(dve, slot, -1, B + 2, 7, B - 2)

        @block.gpsimd
        def _(pool):
            steps = [0]

            def then(ins):
                steps[0] += 1
                ins.then_inc(pool_prep, 1)
                pool.wait_ge(pool_prep, steps[0])

            nc.gpsimd.memset(all_params[:, :], 0).then_inc(params_zeroed, 1)
            nc.gpsimd.memset(ident[:, :], 0.0)
            nc.gpsimd.memset(rows_shift[:, :], 0.0)
            nc.gpsimd.memset(masks16[:, :], 0.0)
            nc.gpsimd.iota(iota_row[:, :], [[1, P]], base=0, channel_multiplier=0,
                           allow_small_or_imprecise_dtypes=True)
            then(nc.gpsimd.iota(iota_col[:, :], [[0, 1]], base=0, channel_multiplier=1,
                                allow_small_or_imprecise_dtypes=True))

            nc.gpsimd.affine_select(ident[:, :], ident[:, :], [[-1, P]], ALU.not_equal, 1.0, base=0,
                                    channel_multiplier=1).then_inc(consts_made, 1)
            for base in (1, -1):
                then(nc.gpsimd.affine_select(rows_shift[:, :], rows_shift[:, :], [[-1, P]], ALU.not_equal, 1.0,
                                             base=base, channel_multiplier=1))
            for to, source in ((0, 1), (P - 1, P - 2)):
                then(nc.gpsimd.affine_select(rows_shift[:, to:to + 1], rows_shift[:, to:to + 1], [[0, 1]],
                                             ALU.not_equal, 2.0, base=-source, channel_multiplier=1))
            for m, (step, mult, op) in enumerate(((-1, 1, ALU.is_ge), (1, -1, ALU.is_ge), (-1, 1, ALU.not_equal))):
                then(nc.gpsimd.affine_select(masks16[:, m * P:(m + 1) * P], masks16[:, m * P:(m + 1) * P], [[step, P]],
                                             op, NEG, base=0, channel_multiplier=mult))
            nc.gpsimd.memset(mark["pool"][:, :], 0.0).then_inc(gconst, 1)
            pool.wait_ge(tables_made, 1)
            pool.wait_ge(tables_in, 16 * 3)
            pool.wait_ge(params_in, PARAMS_IN)

            def inverse_std(h):
                q = h.ring(2)
                pool.wait_ge(vareps_ready, h.upto())
                if h.is_at_least(2):
                    pool.wait_ge(x2_ready, h.upto(2))
                nc.gpsimd.tensor_tensor(rstd[:, q:q + 1], var_eps[:, q:q + 1], minus_half[:, :], ALU.pow
                                        ).then_inc(rstd_ready, 1)

            def columns_and_reaction(h):
                q = h.ring(2)
                pool.wait_ge(x2_ready, h.upto())
                ends = x2[:, q, 2:D:D - 3]
                nc.gpsimd.tensor_tensor(x2[:, q, 0:D + 2:D + 1], ends, ones2[:, :], ALU.mult).then_inc(edges_ready, 1)
                pool.wait_ge(edges_ready, h.upto())
                if h.is_at_least(1):
                    pool.wait_ge(x3_ready, h.upto(1))
                nc.gpsimd.tensor_tensor(neighbours[:, :], x2[:, q, 0:D], x2[:, q, 2:D + 2], ALU.add
                                        ).then_inc(neighbours_ready, 1)
                pool.wait_ge(react_ready, h.upto())
                nc.gpsimd.tensor_tensor(react[:, :], react[:, :], x2[:, q, 1:D + 1], ALU.mult
                                        ).then_inc(react_x2_ready, 1)

            def low_w3_end(c, fresh, wslot):
                column = slice(c.ring(2), c.ring(2) + 1)
                with pool.If(fresh):
                    pool.wait_ge(w3_hi_ready, c.upto() * K)
                    if c.is_at_least(2):
                        pool.wait_ge(out_mm, c.upto(2))
                    pool.wait_ge(w3_lo_ready, c.upto() * (K - 1))
                    piece = bass.ds(wslot * (K * D) + (K - 1) * D, D)
                    nc.gpsimd.tensor_tensor(w3_lo[:, piece], w3s[:, piece], w3_hi[:, piece].bitcast(F32),
                                            ALU.subtract).then_inc(w3_lo_end_ready, 1)
                with pool.Else():
                    pool.wait_ge(w3_lo_ready, c.upto() * (K - 1))
                    nc.gpsimd.tensor_tensor(mark["pool"][:, column], minus_half[:, :], minus_half[:, :], ALU.add
                                            ).then_inc(w3_lo_end_ready, 1)

            def add_b2(s, lang):
                pool.wait_ge(x1_ready, s.upto())
                if s.is_first:
                    pool.wait_ge(b2_in, 16 * 2)
                if s.is_at_least(1):
                    pool.wait_ge(y_ready, s.upto(1))
                nc.gpsimd.tensor_tensor(x1_b2[:, :], x1[:, s.ring(2), :], b2_wide[:, bass.ds(lang * D, D)], ALU.add
                                        ).then_inc(x1_b2_ready, 1)

            def add_beta(s, lang):
                if s.is_first:
                    pool.wait_ge(beta_in, 16)
                if s.is_at_least(2):
                    pool.wait_ge(x2_ready, s.upto(2))
                nc.gpsimd.tensor_tensor(x1_beta[:, s.ring(2), :], x1[:, s.ring(2), :],
                                        beta_wide[:, bass.ds(lang * D, D)], ALU.add).then_inc(x1_beta_ready, 1)

            def slot(s):
                if (s - 1).inside(B):
                    inverse_std(s - 1)
                lang, fresh, wslot = load_params(pool, "pool", s)
                if s.inside(B):
                    add_b2(s, lang)
                if (s - 1).inside(B):
                    columns_and_reaction(s - 1)
                if s.inside(B):
                    add_beta(s, lang)
                if (s - 1).inside(B):
                    low_w3_end(s - 1, fresh, wslot)

            run_slots(pool, slot, 0, B, 5, B - 2)


def kernel(x, itok_B_0_2, itok_B_0_8, condB_zX, condB_zY, condB_zR, itok_B_0_63, L0_cond_W1, L0_cond_b1, L0_cond_v,
           L1_cond_W1, L1_cond_b1, L1_cond_W2, L1_cond_b2, L1_cond_gamma, L1_cond_beta, L3_cond_W, L3_cond_b):
    import concourse.bacc as bacc
    from concourse.bass_utils import run_bass_kernel_spmd

    def tiles(w):
        w = np.asarray(w)
        *lead, rows, cols = w.shape
        w = np.moveaxis(w.reshape(*lead, rows // P, P, cols), -3, -2)
        return np.ascontiguousarray(w.reshape(*lead, P, rows // P * cols))

    x = np.ascontiguousarray(x)
    L, A, D = L1_cond_W2.shape
    arrays = {
        "x": x,
        "xT": tiles(x.transpose(0, 2, 1)),
        "kinds": np.asarray(itok_B_0_2)[:, None],
        "langs": np.asarray(itok_B_0_8)[:, None],
        "zx": np.asarray(condB_zX)[:, None],
        "zy": np.asarray(condB_zY)[:, None],
        "zr": np.asarray(condB_zR)[:, None],
        "cats": np.asarray(itok_B_0_63)[:, None],
        "w1a": tiles(L0_cond_W1),
        "b1a": np.asarray(L0_cond_b1)[:, None],
        "va": np.asarray(L0_cond_v)[:, None],
        "w1l": tiles(L1_cond_W1),
        "b1l": np.ascontiguousarray(np.asarray(L1_cond_b1).T),
        "w2l": np.ascontiguousarray(np.asarray(L1_cond_W2).transpose(1, 0, 2).reshape(A, L * D)),
        "b2l": np.asarray(L1_cond_b2),
        "gamma": np.asarray(L1_cond_gamma),
        "beta": np.asarray(L1_cond_beta),
        "w3": tiles(L3_cond_W),
        "b3": np.asarray(L3_cond_b),
    }
    arrays = {f"in_{k}": np.ascontiguousarray(v) for k, v in arrays.items()}
    nc = bacc.Bacc("TRN2", target_bir_lowering=False, num_devices=1, dynamic_dma_scratch_size=1024)
    args = [nc.dram_tensor(k, v.shape, mybir.dt.from_np(v.dtype), kind="ExternalInput").ap()
            for k, v in arrays.items()]
    out = nc.dram_tensor("out_x", x.shape, F32, kind="ExternalOutput").ap()
    cond_residual_kernel(nc, *args, out)
    r = run_bass_kernel_spmd(nc, [arrays], core_ids=[0])
    return r.results[0]["out_x"]
```
